# Optimizing a Trainium2 kernel written in Bass

```python
import numpy as np
import jax
import jax.numpy as jnp

def _softmax(x, axis=-1):
    return jax.nn.softmax(x, axis=axis)

def _gelu(x):
    return jax.nn.gelu(x, approximate=True)

def _silu(x):
    return jax.nn.silu(x)

def _sigmoid(x):
    return jax.nn.sigmoid(x)

def _layernorm(x, axis=-1, eps=1e-05):
    m = jnp.mean(x, axis=axis, keepdims=True)
    v = jnp.var(x, axis=axis, keepdims=True)
    return (x - m) / jnp.sqrt(v + eps)

def _scatter_add(tgt, idx, src, axis=0):
    return tgt.at[idx].add(src)

def _segment_sum(src, seg, n):
    return jax.ops.segment_sum(src, seg, n)
kernel_name = 'mk_prb_d1_jaxref_r4_a5c8c1'

def setup_inputs(seed: int=0):
    np.random.seed(seed)
    _w = jnp.asarray

    def _L0_attn_setup():
        import jax, jax.numpy as jnp
        import numpy as np
        import math
        NUM_HEADS = 8
        EMB = 256
        HEAD_DIM = 128
        B, T = (1, 1024)

        def sinusoidal_pe(T, d, dtype=jnp.float32):
            pos = jnp.arange(T, dtype=dtype)[:, None]
            inv_freq = jnp.exp(-math.log(10000.0) * jnp.arange(0, d, 2, dtype=dtype) / d)
            ang = pos * inv_freq[None, :]
            pe = jnp.zeros((T, d), dtype=dtype)
            pe = pe.at[:, 0::2].set(jnp.sin(ang))
            pe = pe.at[:, 1::2].set(jnp.cos(ang))
            return pe
        key = jax.random.key(seed)
        ks = jax.random.split(key, 6)
        s = lambda fan_in: 1.0 / math.sqrt(fan_in)
        x = jax.random.normal(ks[0], (B, T, EMB), dtype=jnp.float32)
        Wq = jax.random.normal(ks[1], (EMB, NUM_HEADS * HEAD_DIM), dtype=jnp.float32) * s(EMB)
        bq = jax.random.normal(ks[2], (NUM_HEADS * HEAD_DIM,), dtype=jnp.float32) * s(EMB)
        Wkv = jax.random.normal(ks[3], (EMB, 2 * HEAD_DIM), dtype=jnp.float32) * s(EMB)
        bkv = jax.random.normal(ks[4], (2 * HEAD_DIM,), dtype=jnp.float32) * s(EMB)
        Wo = jax.random.normal(ks[5], (NUM_HEADS * HEAD_DIM, EMB), dtype=jnp.float32) * s(NUM_HEADS * HEAD_DIM)
        return {'x': x, 'Wq': Wq, 'bq': bq, 'Wkv': Wkv, 'bkv': bkv, 'Wo': Wo}
    _L0_attn_in = _L0_attn_setup()

    def _L0_ffn_setup():
        import jax, jax.numpy as jnp
        import numpy as np
        DIM = 256

        def _reference_tuple_inner(x, W_r, W_k, W_v, mu_r, mu_k):
            B, T, C = x.shape
            x_prev = jnp.concatenate([jnp.zeros((B, 1, C), x.dtype), x[:, :-1, :]], axis=1)
            xr = mu_r * x + (1.0 - mu_r) * x_prev
            xk = mu_k * x + (1.0 - mu_k) * x_prev
            r = jax.nn.sigmoid(jnp.einsum('btc,dc->btd', xr, W_r))
            k = jnp.einsum('btc,dc->btd', xk, W_k)
            k_act = jnp.square(jax.nn.relu(k))
            out = r * jnp.einsum('btc,dc->btd', k_act, W_v)
            new_state = x[:, -1, :]
            return (out, new_state)
        key = jax.random.key(seed)
        ks = jax.random.split(key, 6)
        B, T, C = (8, 512, DIM)
        x = jax.random.normal(ks[0], (B, T, C), dtype=jnp.float32)
        s = 1.0 / np.sqrt(C)
        W_r = jax.random.uniform(ks[1], (C, C), jnp.float32, -s, s)
        W_k = jax.random.uniform(ks[2], (C, C), jnp.float32, -s, s)
        W_v = jax.random.uniform(ks[3], (C, C), jnp.float32, -s, s)
        mu_r = jax.random.uniform(ks[4], (C,), jnp.float32)
        mu_k = jax.random.uniform(ks[5], (C,), jnp.float32)
        return {'x': x, 'W_r': W_r, 'W_k': W_k, 'W_v': W_v, 'mu_r': mu_r, 'mu_k': mu_k}
    _L0_ffn_in = _L0_ffn_setup()
    _d = {'L0_attn_x': _L0_attn_in['x'], 'L0_attn_Wq': _L0_attn_in['Wq'], 'L0_attn_bq': _L0_attn_in['bq'], 'L0_attn_Wkv': _L0_attn_in['Wkv'], 'L0_attn_bkv': _L0_attn_in['bkv'], 'L0_attn_Wo': _L0_attn_in['Wo'], 'L0_ffn_W_r': _L0_ffn_in['W_r'], 'L0_ffn_W_k': _L0_ffn_in['W_k'], 'L0_ffn_W_v': _L0_ffn_in['W_v'], 'L0_ffn_mu_r': _L0_ffn_in['mu_r'], 'L0_ffn_mu_k': _L0_ffn_in['mu_k']}
    _x0 = _d['L0_attn_x']
    _d['L0_attn_x'] = jax.random.normal(jax.random.fold_in(jax.random.key(seed), 1), (8, 1024, 256), dtype=_x0.dtype)
    del _x0
    return _d

def reference(L0_attn_x, L0_attn_Wq, L0_attn_bq, L0_attn_Wkv, L0_attn_bkv, L0_attn_Wo, L0_ffn_W_r, L0_ffn_W_k, L0_ffn_W_v, L0_ffn_mu_r, L0_ffn_mu_k):

    def _L0_attn_ref(x, Wq, bq, Wkv, bkv, Wo):
        import jax, jax.numpy as jnp
        import numpy as np
        import math
        NUM_HEADS = 8
        EMB = 256
        HEAD_DIM = 128
        B, T = (1, 1024)

        def sinusoidal_pe(T, d, dtype=jnp.float32):
            pos = jnp.arange(T, dtype=dtype)[:, None]
            inv_freq = jnp.exp(-math.log(10000.0) * jnp.arange(0, d, 2, dtype=dtype) / d)
            ang = pos * inv_freq[None, :]
            pe = jnp.zeros((T, d), dtype=dtype)
            pe = pe.at[:, 0::2].set(jnp.sin(ang))
            pe = pe.at[:, 1::2].set(jnp.cos(ang))
            return pe
        Bsz, Tlen, E = x.shape
        q = (x @ Wq + bq).reshape(Bsz, Tlen, NUM_HEADS, HEAD_DIM)
        kv = x @ Wkv + bkv
        k, v = (kv[..., :HEAD_DIM], kv[..., HEAD_DIM:])
        q = jnp.transpose(q, (0, 2, 1, 3))
        pe = sinusoidal_pe(Tlen, HEAD_DIM, x.dtype)
        q = q + pe[None, None, :, :]
        k = k + pe[None, :, :]
        scale = 1.0 / math.sqrt(HEAD_DIM)
        scores = jnp.einsum('bhqd,bkd->bhqk', q, k) * scale
        causal = jnp.tril(jnp.ones((Tlen, Tlen), dtype=bool))
        scores = jnp.where(causal[None, None, :, :], scores, jnp.finfo(scores.dtype).min)
        probs = jax.nn.softmax(scores, axis=-1)
        attn = jnp.einsum('bhqk,bkd->bhqd', probs, v)
        out = jnp.transpose(attn, (0, 2, 1, 3)).reshape(Bsz, Tlen, NUM_HEADS * HEAD_DIM)
        return out @ Wo

    def _L0_ffn_ref(x, W_r, W_k, W_v, mu_r, mu_k):
        import jax, jax.numpy as jnp
        import numpy as np
        DIM = 256

        def _reference_tuple_inner(x, W_r, W_k, W_v, mu_r, mu_k):
            B, T, C = x.shape
            x_prev = jnp.concatenate([jnp.zeros((B, 1, C), x.dtype), x[:, :-1, :]], axis=1)
            xr = mu_r * x + (1.0 - mu_r) * x_prev
            xk = mu_k * x + (1.0 - mu_k) * x_prev
            r = jax.nn.sigmoid(jnp.einsum('btc,dc->btd', xr, W_r))
            k = jnp.einsum('btc,dc->btd', xk, W_k)
            k_act = jnp.square(jax.nn.relu(k))
            out = r * jnp.einsum('btc,dc->btd', k_act, W_v)
            new_state = x[:, -1, :]
            return (out, new_state)
        return _reference_tuple_inner(x, W_r, W_k, W_v, mu_r, mu_k)[0]
    x = L0_attn_x
    xn = _layernorm(x, axis=-1)
    x = x + _L0_attn_ref(xn, L0_attn_Wq, L0_attn_bq, L0_attn_Wkv, L0_attn_bkv, L0_attn_Wo) + _L0_ffn_ref(xn, L0_ffn_W_r, L0_ffn_W_k, L0_ffn_W_v, L0_ffn_mu_r, L0_ffn_mu_k)
    return x

_drawn_inputs = setup_inputs


def setup_inputs(seed=0):
    import zlib

    import numpy as np

    out = dict(_drawn_inputs(seed))
    spreads = {}
    factors = {'L0_attn_bq': 4.922, 'L0_ffn_W_r': 3.247, 'L0_ffn_mu_r': 6.534}
    for name, (base, spread) in spreads.items():
        noise = np.random.default_rng([zlib.crc32(name.encode()), seed]).standard_normal(out[name].shape)
        drawn = base * np.exp(spread * noise) if base else spread * noise
        out[name] = jnp.asarray(drawn.astype(out[name].dtype))
    for name, factor in factors.items():
        out[name] = (out[name] * factor).astype(out[name].dtype)
    return out
```

```python
import concourse.bass as bass
from concourse import mybir
from contextlib import ExitStack

B, T, E = 8, 1024, 256
H, D = 8, 128
P = 128
CT = E // P
CHUNK = 256
TPC = CHUNK // P
NC = T // CHUNK
NT = T // P
PAIRS = H // 2
STEPS = NT * H
SCALE = float(D) ** -0.5
EPS = 1e-5
MASKED = 1e30
HUGE = 3e38
T_LAG = 3
PV_LAG = 5
XBUF = 4
LAST_IT = STEPS + 6


def fillers():
    at = {it: [] for it in range(LAST_IT)}
    for c in range(NC):
        i = c * TPC * H
        at[i + 1].append(("FK", c, 0))
        at[i + 3].append(("FR", c, 0))
        at[i + 6].append(("FV", c, 0))
        at[i + 13].append(("WO", c, 0))
        if c:
            at[i + 5].append(("WO", c - 1, 1))
        if c < NC - 1:
            at[i + 4].append(("XT", c + 1, 0))
            at[i + 7].append(("KV", c + 1, 0))
            at[i + 8].append(("KT", c + 1, 0))
            for p in range(PAIRS):
                at[i + 9 + p + (p == 3)].append(("Q", c + 1, p))
        else:
            at[i + 8].append(("XT", NC, 0))
            at[STEPS - 1].append(("KV", NC, 0))
            at[STEPS].append(("KT", NC, 0))
            for p in range(PAIRS):
                at[STEPS + p].append(("Q", NC, p))
            at[STEPS + 5].append(("WO", c, 1))
    return at


FILL = fillers()
START = [("XT", 0, 0), ("KV", 0, 0), ("KT", 0, 0)] + [("Q", 0, p) for p in range(PAIRS)]
G_ORDER = [u for it in range(LAST_IT) for u in FILL[it]]
G_INDEX = {u: n for n, u in enumerate(G_ORDER)}
G_START = len(START)
G_BODY = len(G_ORDER)


def t_banks(s):
    n = s // H + 1
    return [(k, min(4, n - k)) for k in range(0, n, 4)]


T_FIRST = [sum(len(t_banks(r)) for r in range(s)) for s in range(STEPS + 1)]
T_BODY = T_FIRST[STEPS]


def build(nc, x_d, wq_d, wkv_d, wo_d, wr_d, wk_d, wv_d, bq_d, bkv_d, mu_d, pet_d, petok_d, out_d):
    F, R = mybir.dt.float32, mybir.dt.float32r
    ALU, ACT = mybir.AluOpType, mybir.ActivationFunctionType

    x_v = x_d.rearrange("b (c t p) e -> (b c) p t e", t=TPC, p=P)
    out_v = out_d.rearrange("b (n p) e -> (b n) p e", p=P)

    with ExitStack() as ctx:
        def sb(name, shape, dt=F):
            return ctx.enter_context(nc.sbuf_tensor(name, shape, dt))

        def pb(name, shape):
            return ctx.enter_context(nc.psum_tensor(name, shape, F))

        def sem(name):
            return ctx.enter_context(nc.semaphore(name))

        wq = [sb(f"wq{i}", [P, CT, H * D], R) for i in range(2)]
        wkv = [sb(f"wkv{i}", [P, CT, 2 * D], R) for i in range(2)]
        wo = [sb(f"wo{i}", [P, H, E], R) for i in range(2)]
        wr = [sb(f"wr{i}", [P, CT, E], R) for i in range(2)]
        wk = [sb(f"wk{i}", [P, CT, E], R) for i in range(2)]
        wv = [sb(f"wv{i}", [P, CT, E], R) for i in range(2)]
        bq = sb("bq", [P, H])
        mu = sb("mu", [P, 4])
        omu = sb("omu", [P, 4])
        bkv = sb("bkv", [P, 2 * D])
        kpos = sb("kpos", [P, NT, D])
        pet = sb("pet", [P, T])
        mask = sb("mask", [P, T])
        ident = sb("ident", [P, P])
        kt = [sb(f"kt{i}", [P, T], R) for i in range(2)]
        v = [sb(f"v{i}", [P, NT, D], R) for i in range(2)]
        xtok = sb("xtok", [P, NC, TPC, E])
        xn = sb("xn", [P, TPC, E])
        stats = sb("stats", [P, TPC, 6])
        mv = sb("mv", [P, TPC, 2])
        rstd = sb("rstd", [P, TPC])
        vare = sb("vare", [P, TPC])
        half = sb("half", [P, TPC])
        xnt = sb("xnt", [P, 2, CT, CHUNK + 1])
        xt = [sb(f"xt{i}", [P, 2, CT, CHUNK], R) for i in range(2)]
        qt = [sb(f"qt{i}", [P, 2, H, CHUNK], R) for i in range(2)]
        qtmp = sb("qtmp", [P, 2, CHUNK])
        mix = sb("mix", [P, CT, CHUNK])
        mh = [sb(f"mh{i}", [P, CT, CHUNK], R) for i in range(2)]
        ka = sb("ka", [P, CT, CHUNK])
        kh = [sb(f"kh{i}", [P, CT, CHUNK], R) for i in range(2)]
        gate = sb("gate", [P, TPC, E])
        gated = sb("gated", [P, TPC, E])
        X = sb("X", [P, XBUF, T])
        bias = sb("bias", [P, XBUF])
        total = sb("total", [P, XBUF])
        rec = sb("rec", [P, XBUF])
        pt = [sb(f"pt{i}", [P, 2, NT, 2 * P], R) for i in range(2)]
        ot = [sb(f"ot{i}", [P, H, P], R) for i in range(2)]

        pS = [pb(f"pS{i}", [P, 2, 512]) for i in range(2)]
        pT = [pb(f"pT{i}", [P, 512]) for i in range(2)]
        pO = pb("pO", [P, 512])
        pG = pb("pG", [P, 512])

        x_loaded = [sem(f"x_loaded{c}") for c in range(NC)]
        small_loaded = sem("small_loaded")
        wa_loaded = sem("wa_loaded")
        wo_loaded = sem("wo_loaded")
        wa_hi = sem("wa_hi")
        wa_lo = sem("wa_lo")
        wo_hi = sem("wo_hi")
        wo_lo = sem("wo_lo")
        consts = sem("consts")
        kpos_ready = sem("kpos_ready")
        g_filled = sem("g_filled")
        g_free = sem("g_free")
        bn_done = sem("bn_done")
        var_ready = sem("var_ready")
        rstd_ready = sem("rstd_ready")
        xn_ready = sem("xn_ready")
        xnt_ready = sem("xnt_ready")
        xnt_kept = sem("xnt_kept")
        xt_hi = sem("xt_hi")
        xt_ready = sem("xt_ready")
        kv_ready = sem("kv_ready")
        kt_hi = sem("kt_hi")
        kt_ready = sem("kt_ready")
        v_hi = sem("v_hi")
        v_ready = sem("v_ready")
        q_sum = sem("q_sum")
        q_hi = sem("q_hi")
        q_ready = sem("q_ready")
        prev_ready = sem("prev_ready")
        mix_ready = sem("mix_ready")
        mix_hi = sem("mix_hi")
        mix_split = sem("mix_split")
        relu_ready = sem("relu_ready")
        square_ready = sem("square_ready")
        ka_hi = sem("ka_hi")
        ka_split = sem("ka_split")
        gexp_ready = sem("gexp_ready")
        gate_den = sem("gate_den")
        gate_ready = sem("gate_ready")
        gated_ready = sem("gated_ready")
        mixed = sem("mixed")
        out_ready = sem("out_ready")
        stored = [sem(f"stored{c}") for c in range(NC)]
        s_filled = sem("s_filled")
        masked = sem("masked")
        exp_done = sem("exp_done")
        rec_ready = sem("rec_ready")
        normed = sem("normed")
        t_filled = sem("t_filled")
        t_hi = sem("t_hi")
        t_lo = sem("t_lo")
        pv_done = sem("pv_done")
        o_hi = sem("o_hi")
        o_lo = sem("o_lo")
        dve_passed = sem("dve_passed")
        pool_passed = sem("pool_passed")

        stage = X[:, :, :].rearrange("p a n -> p (a n)")
        SIZES = [("wq", CT * H * D), ("wkv", CT * 2 * D), ("wr", CT * E), ("wk", CT * E), ("wv", CT * E)]
        OFF = {}
        off = 0
        for name, n in SIZES:
            OFF[name] = (off, n)
            off += n
        W = {"wq": wq, "wkv": wkv, "wr": wr, "wk": wk, "wv": wv}

        def staged(name):
            a, n = OFF[name]
            return stage[:, a:a + n].rearrange("p (t n) -> p t n", t=CT)

        wo_stage = stage[:, 0:H * E].rearrange("p (t n) -> p t n", t=H)

        def g_use(b, u):
            return START.index(u) if b is None else G_START + b * G_BODY + G_INDEX[u]

        def chunk_no(b, c):
            return 0 if b is None else b * NC + c

        block = ctx.enter_context(nc.Block())

        @block.sync
        def _(sp):
            sp.dma_start(xtok[:, 0, :, :], x_v[0, :, :, :]).then_inc(x_loaded[0], 16)
            for name, src in (("wkv", wkv_d), ("wq", wq_d), ("wk", wk_d), ("wr", wr_d), ("wv", wv_d)):
                sp.dma_start(staged(name), src.rearrange("(t p) n -> p t n", p=P)).then_inc(wa_loaded, 16)
            sp.wait_ge(wa_lo, len(SIZES))
            sp.dma_start(wo_stage, wo_d.rearrange("(t p) n -> p t n", p=P)).then_inc(wo_loaded, 16)
            for c in range(1, NC):
                sp.dma_start(xtok[:, c, :, :], x_v[c, :, :, :]).then_inc(x_loaded[c], 16)

            def store(b, c, t):
                sp.wait_ge(out_ready, b * NT + c * TPC + t + 1)
                sp.dma_start(out_v[bass.ds(b * NT + c * TPC + t, 1), :, :].rearrange("a p e -> (a p) e"),
                             xtok[:, c, t, :]).then_inc(stored[c], 16)

            with sp.Fori(0, B) as b:
                for c in range(NC):
                    for t in range(TPC):
                        store(b, c, t)
                    sp.wait_ge(stored[c], (b + 1) * (16 * TPC))
                    sp.dma_start(xtok[:, c, :, :],
                                 x_v[bass.ds((b * NC + NC + c) % (B * NC), 1), :, :, :]
                                 .rearrange("a p t e -> (a p) t e")).then_inc(x_loaded[c], 16)
            for c in range(NC):
                sp.wait_ge(stored[c], 16 * TPC * B)
                sp.wait_ge(x_loaded[c], 16 * (B + 1))

        @block.gpsimd
        def _(pool):
            pool.dma_start(bkv[:, :], bkv_d).then_inc(small_loaded, 16)
            pool.dma_start(kpos[:, :, :], petok_d.rearrange("(n p) d -> p n d", p=P)).then_inc(small_loaded, 16)
            pool.dma_start(bq[:, :], bq_d).then_inc(small_loaded, 16)
            pool.dma_start(mu[:, :], mu_d).then_inc(small_loaded, 16)
            pool.dma_start(pet[:, :], pet_d).then_inc(small_loaded, 16)
            nc.gpsimd.memset(ident[:, :], 0.0).then_inc(consts, 1)
            nc.gpsimd.memset(half[:, :], -0.5).then_inc(consts, 1)
            nc.gpsimd.memset(mask[:, :], 0.0).then_inc(consts, 1)
            pool.wait_ge(consts, 3)
            nc.gpsimd.affine_select(out=ident[:, :], in_=ident[:, :], compare_op=ALU.not_equal, fill=1.0,
                                    base=0, pattern=[[-1, P]], channel_multiplier=1).then_inc(consts, 1)
            tri = mask[:, T - P:T]
            nc.gpsimd.affine_select(out=tri, in_=tri, compare_op=ALU.is_ge, fill=MASKED,
                                    base=0, pattern=[[-1, P]], channel_multiplier=1).then_inc(consts, 1)

            def inv_std(n):
                pool.wait_ge(var_ready, n + 1)
                nc.gpsimd.tensor_tensor(rstd[:, :], vare[:, :], half[:, :], ALU.pow).then_inc(rstd_ready, 1)

            def split_xt(n, slot):
                pool.wait_ge(xnt_ready, n + 1)
                xs = xnt[:, slot, :, 1:CHUNK + 1]
                pool.sem_inc(pool_passed, 1)
                nc.gpsimd.tensor_copy(xt[0][:, slot, :, :], xs).then_inc(xt_hi, 1)
                pool.wait_ge(xt_hi, n + 1)
                nc.gpsimd.tensor_tensor(xt[1][:, slot, :, :], xs, xt[0][:, slot, :, :].bitcast(F),
                                        ALU.subtract).then_inc(xt_ready, 1)

            def split_v(n, c):
                pool.wait_ge(v_hi, n + 1)
                tiles = slice(c * TPC, (c + 1) * TPC)
                nc.gpsimd.tensor_tensor(v[1][:, tiles, :], xn[:, :, D:2 * D], v[0][:, tiles, :].bitcast(F),
                                        ALU.subtract).then_inc(v_ready, 1)

            def split_q(n, slot, p):
                pool.wait_ge(q_hi, n * PAIRS + p + 1)
                hs = slice(2 * p, 2 * p + 2)
                nc.gpsimd.tensor_tensor(qt[1][:, slot, hs, :], qtmp[:, :, :], qt[0][:, slot, hs, :].bitcast(F),
                                        ALU.subtract).then_inc(q_ready, 1)

            def split_mix(b, c, turn):
                n = (b * NC + c) * 2 + turn
                if turn:
                    pool.wait_ge(g_filled, g_use(b, ("FK", c, 0)) + 1)
                elif c:
                    pool.wait_ge(g_filled, g_use(b, ("FR", c - 1, 0)) + 1)
                pool.wait_ge(mix_ready, n * CT + CT)
                pool.sem_inc(pool_passed, 1)
                nc.gpsimd.tensor_copy(mh[0][:, :, :], mix[:, :, :]).then_inc(mix_hi, 1)
                pool.wait_ge(mix_hi, n + 1)
                nc.gpsimd.tensor_tensor(mh[1][:, :, :], mix[:, :, :], mh[0][:, :, :].bitcast(F),
                                        ALU.subtract).then_inc(mix_split, 1)

            def square(b, c):
                n = b * NC + c
                pool.wait_ge(relu_ready, n + 1)
                nc.gpsimd.tensor_tensor(ka[:, :, :], ka[:, :, :], ka[:, :, :], ALU.mult).then_inc(square_ready, 1)
                pool.wait_ge(square_ready, n + 1)
                pool.sem_inc(pool_passed, 1)
                nc.gpsimd.tensor_copy(kh[0][:, :, :], ka[:, :, :]).then_inc(ka_hi, 1)
                pool.wait_ge(ka_hi, n + 1)
                nc.gpsimd.tensor_tensor(kh[1][:, :, :], ka[:, :, :], kh[0][:, :, :].bitcast(F),
                                        ALU.subtract).then_inc(ka_split, 1)

            inv_std(0)
            split_xt(0, 0)
            split_v(0, 0)
            for p in range(PAIRS):
                split_q(0, 0, p)

            with pool.Fori(0, B) as b:
                for it in range(LAST_IT):
                    s = it - 1
                    if 0 <= s < STEPS:
                        w = (s // H + 1) * P
                        j = s % XBUF
                        pool.wait_ge(rec_ready, b * STEPS + s + 1)
                        pool.sem_inc(pool_passed, 1)
                        nc.gpsimd.tensor_scalar(X[:, j, 0:w], X[:, j, 0:w], rec[:, j:j + 1], 1.0,
                                                ALU.mult, ALU.mult).then_inc(normed, 1)
                    if it < STEPS and it % (TPC * H) == 0:
                        inv_std(chunk_no(b, it // (TPC * H) + 1))
                    if it < STEPS and it % (TPC * H) in (0, 1):
                        split_mix(b, it // (TPC * H), it % (TPC * H))
                    for kind, c, p in FILL[it]:
                        if kind == "XT":
                            split_xt(chunk_no(b, c), c % 2)
                        elif kind == "KT" and c < NC:
                            split_v(chunk_no(b, c), c)
                        elif kind == "Q":
                            split_q(chunk_no(b, c), c % 2, p)
                        elif kind == "FK":
                            square(b, c)
                        elif kind == "FV":
                            pool.wait_ge(gated_ready, b * NC + c + 1)
                            nc.gpsimd.tensor_tensor(xtok[:, c, :, :], xtok[:, c, :, :], gated[:, :, :],
                                                    ALU.add).then_inc(mixed, 1)
                    if it == STEPS + 4:
                        split_v(chunk_no(b, NC), 0)

        @block.scalar
        def _(act):
            for n, (name, _) in enumerate((("wkv", 0), ("wq", 0), ("wk", 0), ("wr", 0), ("wv", 0))):
                if n == 0:
                    act.wait_ge(wa_loaded, 16 * len(SIZES))
                nc.scalar.copy(W[name][0][:, :, :], staged(name)).then_inc(wa_hi, 1)

            def xt_out(b, c):
                n = chunk_no(b, c)
                slot = c % 2
                act.wait_ge(g_filled, g_use(b, ("XT", c, 0)) + 1)
                nc.scalar.activation(xnt[:, slot, :, 0:1], xnt[:, 1 - slot, :, CHUNK:CHUNK + 1], ACT.Copy,
                                     scale=float(c % NC > 0)).then_inc(xnt_kept, 1)
                nc.scalar.copy(xnt[:, slot, :, 1:CHUNK + 1],
                               pG[:, :].rearrange("p (t n) -> p t n", t=CT)).then_inc(xnt_ready, 1)

            def kt_out(b, c):
                act.wait_ge(g_filled, g_use(b, ("KT", c, 0)) + 1)
                k0 = (c % NC) * CHUNK
                nc.scalar.activation(kt[0][:, k0:k0 + CHUNK], pG[:, 0:CHUNK], ACT.Copy, scale=-1.0
                                     ).then_inc(kt_hi, 1)

            def v_out(b, c):
                act.wait_ge(kv_ready, 2 * chunk_no(b, c) + 2)
                tiles = slice((c % NC) * TPC, (c % NC + 1) * TPC)
                nc.scalar.copy(v[0][:, tiles, :], xn[:, :, D:2 * D]).then_inc(v_hi, 1)

            def q_out(b, c, p):
                act.wait_ge(q_sum, (chunk_no(b, c) * PAIRS + p) * 2 + 2)
                nc.scalar.copy(qt[0][:, c % 2, 2 * p:2 * p + 2, :], qtmp[:, :, :]).then_inc(q_hi, 1)

            xt_out(None, 0)
            kt_out(None, 0)
            v_out(None, 0)
            for p in range(PAIRS):
                q_out(None, 0, p)
            act.wait_ge(wo_loaded, 16)
            nc.scalar.copy(wo[0][:, :, :], wo_stage).then_inc(wo_hi, 1)

            with act.Fori(0, B) as b:
                for it in range(LAST_IT):
                    s = it - 1
                    if 0 <= s < STEPS:
                        w = (s // H + 1) * P
                        j = s % XBUF
                        act.wait_ge(masked, b * STEPS + s + 1)
                        nc.scalar.activation(X[:, j, 0:w], X[:, j, 0:w], ACT.Exp, bias=bias[:, j:j + 1],
                                             scale=-1.0, accum_out=total[:, j:j + 1]).then_inc(exp_done, 1)
                    for kind, c, p in FILL[it]:
                        if kind == "XT":
                            xt_out(b, c)
                        elif kind == "KT":
                            kt_out(b, c)
                            if c < NC:
                                v_out(b, c)
                        elif kind == "FK":
                            act.wait_ge(g_filled, g_use(b, ("FK", c, 0)) + 1)
                            nc.scalar.activation(ka[:, :, :], pG[:, :].rearrange("p (t n) -> p t n", t=CT),
                                                 ACT.Relu).then_inc(relu_ready, 1)
                        elif kind == "FR":
                            act.wait_ge(g_filled, g_use(b, ("FR", c, 0)) + 1)
                            nc.scalar.activation(gate[:, :, :], pG[:, :].rearrange("p (t n) -> p t n", t=TPC),
                                                 ACT.Exp, scale=-1.0).then_inc(gexp_ready, 1)
                    first = it - PV_LAG
                    if 0 <= first < STEPS and first % 2 == 0:
                        pair = first // 2
                        act.wait_ge(pv_done, b * (STEPS // 2) + pair + 1)
                        h = first % H
                        nc.scalar.copy(ot[0][:, h:h + 2, :],
                                       pO[:, 0:2 * P].rearrange("p (h q) -> p h q", h=2)).then_inc(o_hi, 1)
                    s = it - T_LAG
                    if 0 <= s < STEPS:
                        half_q = slice((s % 2) * P, (s % 2 + 1) * P)
                        for m, (k, nk) in enumerate(t_banks(s)):
                            u = T_FIRST[s] + m
                            act.wait_ge(t_filled, b * T_BODY + u + 1)
                            nc.scalar.copy(pt[0][:, (s // 2) % 2, k:k + nk, half_q],
                                           pT[u % 2][:, 0:nk * P].rearrange("p (k q) -> p k q", k=nk)
                                           ).then_inc(t_hi, 1)
                    for kind, c, p in FILL[it]:
                        if kind == "Q":
                            q_out(b, c, p)
                    if it == STEPS + 4:
                        v_out(b, NC)

        @block.vector
        def _(dve):
            def norm_stats(n, slot, b):
                dve.wait_ge(x_loaded[slot], 16 if b is None else 16 * ((b + 1) if slot else (b + 2)))
                for t in range(TPC):
                    nc.vector.bn_stats(stats[:, t, :], xtok[:, slot, t, :]).then_inc(bn_done, 1)
                dve.wait_ge(bn_done, n * 2 * TPC + TPC)
                dve.sem_inc(dve_passed, 1)
                for t in range(TPC):
                    nc.vector.bn_aggr(mv[:, t, :], stats[:, t, :]).then_inc(bn_done, 1)
                dve.wait_ge(bn_done, n * 2 * TPC + 2 * TPC)
                nc.vector.tensor_scalar_add(vare[:, :], mv[:, :, 1], EPS).then_inc(var_ready, 1)

            def norm_apply(n, slot):
                dve.wait_ge(rstd_ready, n + 1)
                for t in range(TPC):
                    nc.vector.tensor_scalar(xn[:, t, :], xtok[:, slot, t, :], mv[:, t, 0:1], rstd[:, t:t + 1],
                                            ALU.subtract, ALU.mult).then_inc(xn_ready, 1)

            def kv_out(b, c):
                n = chunk_no(b, c)
                dve.wait_ge(g_filled, g_use(b, ("KV", c, 0)) + 1)
                g = pG[:, :].rearrange("p (t n) -> p t n", t=TPC)
                tiles = slice((c % NC) * TPC, (c % NC + 1) * TPC)
                nc.vector.tensor_tensor(xn[:, :, 0:D], g[:, :, 0:D], kpos[:, tiles, :], ALU.add
                                        ).then_inc(kv_ready, 1)
                nc.vector.tensor_tensor(xn[:, :, D:2 * D], g[:, :, D:2 * D],
                                        bkv[:, D:2 * D].rearrange("p (a n) -> p a n", a=1).broadcast_to((P, TPC, D)),
                                        ALU.add).then_inc(kv_ready, 1)

            def kt_out(b, c):
                dve.wait_ge(kt_hi, chunk_no(b, c) + 1)
                k0 = (c % NC) * CHUNK
                nc.vector.scalar_tensor_tensor(kt[1][:, k0:k0 + CHUNK], pG[:, 0:CHUNK], -1.0,
                                               kt[0][:, k0:k0 + CHUNK].bitcast(F), ALU.mult, ALU.subtract
                                               ).then_inc(kt_ready, 1)

            def q_out(b, c, p):
                n = chunk_no(b, c)
                dve.wait_ge(g_filled, g_use(b, ("Q", c, p)) + 1)
                if b is not None:
                    dve.wait_ge(q_ready, n * PAIRS + p)
                elif p:
                    dve.wait_ge(q_ready, p)
                t0 = (c % NC) * CHUNK
                for i in range(2):
                    h = 2 * p + i
                    nc.vector.scalar_tensor_tensor(qtmp[:, i, :], pG[:, i * CHUNK:(i + 1) * CHUNK], bq[:, h:h + 1],
                                                   pet[:, t0:t0 + CHUNK], ALU.add, ALU.add).then_inc(q_sum, 1)

            def token_mix(b, c, which):
                n = (b * NC + c) * 2 + (1 - which)
                x_now = xnt[:, c % 2, :, 1:CHUNK + 1]
                x_before = xnt[:, c % 2, :, 0:CHUNK]
                for t in range(CT):
                    m = which * CT + t
                    nc.vector.tensor_scalar(mix[:, t, :], x_before[:, t, :], omu[:, m:m + 1], None, ALU.mult
                                            ).then_inc(prev_ready, 1)
                dve.wait_ge(prev_ready, n * CT + CT)
                for t in range(CT):
                    m = which * CT + t
                    nc.vector.scalar_tensor_tensor(mix[:, t, :], x_now[:, t, :], mu[:, m:m + 1], mix[:, t, :],
                                                   ALU.mult, ALU.add).then_inc(mix_ready, 1)

            norm_stats(0, 0, None)
            dve.wait_ge(small_loaded, 80)
            nc.vector.tensor_scalar(omu[:, :], mu[:, :], -1.0, 1.0, ALU.mult, ALU.add).then_inc(kpos_ready, 1)
            nc.vector.tensor_tensor(kpos[:, :, :], kpos[:, :, :],
                                    bkv[:, 0:D].rearrange("p (a n) -> p a n", a=1).broadcast_to((P, NT, D)),
                                    ALU.add).then_inc(kpos_ready, 1)
            nc.vector.memset(xnt[:, 1, :, CHUNK:CHUNK + 1], 0.0).then_inc(kpos_ready, 1)
            norm_apply(0, 0)
            for n, name in enumerate(("wkv", "wq", "wk", "wr", "wv")):
                dve.wait_ge(wa_hi, n + 1)
                nc.vector.tensor_tensor(W[name][1][:, :, :], staged(name), W[name][0][:, :, :].bitcast(F),
                                        ALU.subtract).then_inc(wa_lo, 1)
            dve.wait_ge(kpos_ready, 3)
            kv_out(None, 0)
            kt_out(None, 0)
            for p in range(PAIRS):
                q_out(None, 0, p)
            dve.wait_ge(wo_hi, 1)
            nc.vector.tensor_tensor(wo[1][:, :, :], wo_stage, wo[0][:, :, :].bitcast(F), ALU.subtract
                                    ).then_inc(wo_lo, 1)
            dve.wait_ge(wo_lo, 1)
            dve.wait_ge(consts, 5)

            with dve.Fori(0, B) as b:
                for it in range(LAST_IT):
                    s = it
                    if s < STEPS:
                        qi = s // H
                        w = (qi + 1) * P
                        j = s % XBUF
                        if qi < 4:
                            scores = pS[s % 2][:, 0, 0:w]
                            m = mask[:, T - w:T]
                            o = X[:, j, 0:w]
                        else:
                            scores = pS[s % 2][:, :, 0:w // 2]
                            m = mask[:, T - w:T].rearrange("p (a n) -> p a n", a=2)
                            o = X[:, j, 0:w].rearrange("p (a n) -> p a n", a=2)
                        if s >= XBUF:
                            dve.wait_ge(t_filled, b * T_BODY + T_FIRST[s - XBUF + 1])
                        dve.wait_ge(s_filled, b * STEPS + s + 1)
                        dve.sem_inc(dve_passed, 1)
                        nc.vector.tensor_tensor_reduce(out=o, in0=scores, in1=m, scale=SCALE, scalar=HUGE,
                                                       op0=ALU.add, op1=ALU.min,
                                                       accum_out=bias[:, j:j + 1]).then_inc(masked, 1)
                    s = it - 1
                    if 0 <= s < STEPS:
                        j = s % XBUF
                        dve.wait_ge(exp_done, b * STEPS + s + 1)
                        nc.vector.reciprocal(rec[:, j:j + 1], total[:, j:j + 1]).then_inc(rec_ready, 1)
                    if it < STEPS and it % (TPC * H) == 0:
                        c = it // (TPC * H)
                        dve.wait_ge(xnt_ready, b * NC + c + 1)
                        if c:
                            dve.wait_ge(mix_split, (b * NC + c) * 2)
                        token_mix(b, c, 1)
                        norm_stats(b * NC + c + 1, (c + 1) % NC, b)
                    if it < STEPS and it % (TPC * H) == 1:
                        c = it // (TPC * H)
                        dve.wait_ge(mix_split, (b * NC + c) * 2 + 1)
                        token_mix(b, c, 0)
                    if it < STEPS and it % (TPC * H) == 2:
                        c = it // (TPC * H)
                        dve.wait_ge(v_ready, b * NC + c + 1)
                        norm_apply(b * NC + c + 1, (c + 1) % NC)
                    for kind, c, p in FILL[it]:
                        if kind == "KV":
                            kv_out(b, c)
                        elif kind == "KT":
                            kt_out(b, c)
                        elif kind == "Q":
                            q_out(b, c, p)
                        elif kind == "FR":
                            n = b * NC + c
                            dve.wait_ge(gexp_ready, n + 1)
                            nc.vector.tensor_scalar_add(gate[:, :, :], gate[:, :, :], 1.0).then_inc(gate_den, 1)
                            dve.wait_ge(gate_den, n + 1)
                            nc.vector.reciprocal(gate[:, :, :], gate[:, :, :]).then_inc(gate_ready, 1)
                        elif kind == "FV":
                            n = b * NC + c
                            dve.wait_ge(gate_ready, n + 1)
                            dve.wait_ge(g_filled, g_use(b, ("FV", c, 0)) + 1)
                            nc.vector.tensor_tensor(gated[:, :, :], pG[:, :].rearrange("p (t n) -> p t n", t=TPC),
                                                    gate[:, :, :], ALU.mult).then_inc(gated_ready, 1)
                        elif kind == "WO":
                            dve.wait_ge(mixed, b * NC + c + 1)
                            dve.wait_ge(g_filled, g_use(b, ("WO", c, p)) + 1)
                            nc.vector.tensor_tensor(xtok[:, c, p, :], pG[:, 0:E], xtok[:, c, p, :], ALU.add
                                                    ).then_inc(out_ready, 1)
                    first = it - PV_LAG
                    if 0 <= first < STEPS and first % 2 == 0:
                        pair = first // 2
                        dve.wait_ge(o_hi, b * (STEPS // 2) + pair + 1)
                        h = first % H
                        nc.vector.tensor_tensor(ot[1][:, h:h + 2, :],
                                                pO[:, 0:2 * P].rearrange("p (h q) -> p h q", h=2),
                                                ot[0][:, h:h + 2, :].bitcast(F), ALU.subtract).then_inc(o_lo, 1)
                    s = it - T_LAG
                    if 0 <= s < STEPS:
                        half_q = slice((s % 2) * P, (s % 2 + 1) * P)
                        for m, (k, nk) in enumerate(t_banks(s)):
                            u = T_FIRST[s] + m
                            dve.wait_ge(t_hi, b * T_BODY + u + 1)
                            nc.vector.tensor_tensor(pt[1][:, (s // 2) % 2, k:k + nk, half_q],
                                                    pT[u % 2][:, 0:nk * P].rearrange("p (k q) -> p k q", k=nk),
                                                    pt[0][:, (s // 2) % 2, k:k + nk, half_q].bitcast(F),
                                                    ALU.subtract).then_inc(t_lo, 1)

        @block.tensor
        def _(pe):
            PASSES = ((0, 0), (0, 1), (1, 0))

            def product(out, terms, start=True):
                n = len(terms) * len(PASSES)
                k = 0
                for a, m in terms:
                    for i, j in PASSES:
                        last = nc.tensor.matmul(out, a[i], m[j], start=start and k == 0, stop=k == n - 1)
                        k += 1
                return last

            def g_turn(b, u):
                n = START.index(u) if b is None else None
                if b is None:
                    if n:
                        pe.wait_ge(g_free_of(START[n - 1])[0], g_free_of(START[n - 1])[1](None, START[n - 1]))
                    return
                k = G_INDEX[u]
                if k:
                    before = G_ORDER[k - 1]
                    pe.wait_ge(g_free_of(before)[0], g_free_of(before)[1](b, before))

            def g_free_of(u):
                return {
                    "XT": (xnt_ready, lambda b, u: chunk_no(b, u[1]) + 1),
                    "KV": (kv_ready, lambda b, u: 2 * chunk_no(b, u[1]) + 2),
                    "KT": (kt_ready, lambda b, u: chunk_no(b, u[1]) + 1),
                    "Q": (q_sum, lambda b, u: (chunk_no(b, u[1]) * PAIRS + u[2]) * 2 + 2),
                    "FK": (relu_ready, lambda b, u: b * NC + u[1] + 1),
                    "FR": (gexp_ready, lambda b, u: b * NC + u[1] + 1),
                    "FV": (gated_ready, lambda b, u: b * NC + u[1] + 1),
                    "WO": (out_ready, lambda b, u: b * NT + u[1] * TPC + u[2] + 1),
                }[u[0]]

            def fill(b, u):
                kind, c, p = u
                g_turn(b, u)
                n = chunk_no(b, c)
                slot = c % 2
                if kind == "XT":
                    pe.wait_ge(xn_ready, n * TPC + TPC)
                    for ct in range(CT):
                        for t in range(TPC):
                            o = ct * CHUNK + t * P
                            last = nc.tensor.transpose(pG[:, o:o + P], xn[:, t, ct * P:(ct + 1) * P], ident[:, :])
                elif kind == "KV":
                    pe.wait_ge(xt_ready, n + 1)
                    for t in range(TPC):
                        last = product(pG[:, t * 2 * D:(t + 1) * 2 * D],
                                       [([x[:, slot, ct, t * P:(t + 1) * P] for x in xt],
                                         [w[:, ct, :] for w in wkv]) for ct in range(CT)])
                elif kind == "KT":
                    pe.wait_ge(kv_ready, 2 * n + 2)
                    for t in range(TPC):
                        last = nc.tensor.transpose(pG[:, t * P:(t + 1) * P], xn[:, t, 0:D], ident[:, :])
                elif kind == "Q":
                    for i in range(2):
                        h = 2 * p + i
                        last = product(pG[:, i * CHUNK:(i + 1) * CHUNK],
                                       [([w[:, ct, h * D:(h + 1) * D] for w in wq],
                                         [x[:, slot, ct, :] for x in xt]) for ct in range(CT)])
                elif kind == "FK":
                    pe.wait_ge(mix_split, (b * NC + c) * 2 + 1)
                    for j in range(CT):
                        last = product(pG[:, j * CHUNK:(j + 1) * CHUNK],
                                       [([w[:, ct, j * P:(j + 1) * P] for w in wk],
                                         [m[:, ct, :] for m in mh]) for ct in range(CT)])
                elif kind == "FR":
                    pe.wait_ge(mix_split, (b * NC + c) * 2 + 2)
                    for t in range(TPC):
                        last = product(pG[:, t * E:(t + 1) * E],
                                       [([m[:, ct, t * P:(t + 1) * P] for m in mh],
                                         [w[:, ct, :] for w in wr]) for ct in range(CT)])
                elif kind == "FV":
                    pe.wait_ge(ka_split, b * NC + c + 1)
                    for t in range(TPC):
                        last = product(pG[:, t * E:(t + 1) * E],
                                       [([m[:, ct, t * P:(t + 1) * P] for m in kh],
                                         [w[:, ct, :] for w in wv]) for ct in range(CT)])
                elif kind == "WO":
                    pe.wait_ge(o_lo, (b * NT + c * TPC + p + 1) * PAIRS)
                    last = product(pG[:, 0:E], [([o[:, h, :] for o in ot], [w[:, h, :] for w in wo])
                                                for h in range(H)])
                last.then_inc(g_filled, 1)

            pe.wait_ge(consts, 5)
            fill(None, START[0])
            pe.wait_ge(wa_lo, len(SIZES))
            for u in START[1:]:
                fill(None, u)
            pe.wait_ge(wo_lo, 1)

            with pe.Fori(0, B) as b:
                for it in range(LAST_IT):
                    s = it
                    if s < STEPS:
                        qi, h = s // H, s % H
                        c, t = qi // TPC, qi % TPC
                        w = (qi + 1) * P
                        if s % (TPC * H) == 0:
                            pe.wait_ge(kt_ready, b * NC + c + 1)
                            pe.wait_ge(q_ready, (b * NC + c + 1) * PAIRS)
                        if s >= 2:
                            pe.wait_ge(masked, b * STEPS + s - 1)
                        n = 1 if qi < 4 else 2
                        wn = w // n
                        for a in range(n):
                            last = product(pS[s % 2][:, a, 0:wn],
                                           [([q[:, c % 2, h, t * P:(t + 1) * P] for q in qt],
                                             [k[:, a * wn:(a + 1) * wn] for k in kt])])
                        last.then_inc(s_filled, 1)
                    for u in FILL[it]:
                        fill(b, u)
                    first = it - PV_LAG
                    if 0 <= first < STEPS and first % 2 == 0:
                        pair = first // 2
                        nk = first // H + 1
                        if first % (TPC * H) == 0:
                            pe.wait_ge(v_ready, b * NC + first // (TPC * H) + 1)
                        if pair:
                            pe.wait_ge(o_lo, b * (STEPS // 2) + pair)
                        pe.wait_ge(t_lo, b * T_BODY + T_FIRST[first + 2])
                        last = product(pO[:, 0:2 * P],
                                       [([x[:, k, :] for x in v], [x[:, pair % 2, k, :] for x in pt])
                                        for k in range(nk)])
                        last.then_inc(pv_done, 1)
                    s = it - T_LAG
                    if 0 <= s < STEPS:
                        pe.wait_ge(normed, b * STEPS + s + 1)
                        for m, (k, nk) in enumerate(t_banks(s)):
                            u = T_FIRST[s] + m
                            if u >= 2:
                                pe.wait_ge(t_lo, b * T_BODY + u - 1)
                            for i in range(nk):
                                last = nc.tensor.transpose(pT[u % 2][:, i * P:(i + 1) * P],
                                                           X[:, s % XBUF, (k + i) * P:(k + i + 1) * P],
                                                           ident[:, :])
                            last.then_inc(t_filled, 1)


def _positions():
    import numpy as np
    pos = np.arange(T, dtype=np.float32)[:, None]
    inv = np.exp(np.float32(-np.log(10000.0)) * np.arange(0, D, 2, dtype=np.float32) / np.float32(D))
    ang = (pos * inv.astype(np.float32)[None, :]).astype(np.float32)
    pe = np.zeros((T, D), np.float32)
    pe[:, 0::2] = np.sin(ang)
    pe[:, 1::2] = np.cos(ang)
    return pe


def kernel(L0_attn_x, L0_attn_Wq, L0_attn_bq, L0_attn_Wkv, L0_attn_bkv, L0_attn_Wo, L0_ffn_W_r, L0_ffn_W_k,
           L0_ffn_W_v, L0_ffn_mu_r, L0_ffn_mu_k):
    import numpy as np
    import concourse.bacc as bacc
    from concourse.bass_utils import run_bass_kernel_spmd

    pe = _positions()
    arrays = {
        "x": np.asarray(L0_attn_x),
        "wq": np.asarray(L0_attn_Wq),
        "wkv": np.asarray(L0_attn_Wkv),
        "wo": np.asarray(L0_attn_Wo),
        "wr": np.asarray(L0_ffn_W_r).T,
        "wk": np.asarray(L0_ffn_W_k).T,
        "wv": np.asarray(L0_ffn_W_v).T,
        "bq": np.asarray(L0_attn_bq).reshape(H, D).T,
        "bkv": np.tile(np.asarray(L0_attn_bkv)[None, :], (P, 1)),
        "mu": np.concatenate([np.asarray(L0_ffn_mu_r).reshape(CT, P), np.asarray(L0_ffn_mu_k).reshape(CT, P)]).T,
        "pet": pe.T,
        "petok": pe,
    }
    arrays = {name: np.ascontiguousarray(a) for name, a in arrays.items()}
    nc = bacc.Bacc("TRN2", target_bir_lowering=False, num_devices=1)
    args = [nc.dram_tensor(name + "_dram", a.shape, mybir.dt.from_np(a.dtype), kind="ExternalInput").ap()
            for name, a in arrays.items()]
    out = nc.dram_tensor("out_dram", (B, T, E), mybir.dt.float32, kind="ExternalOutput").ap()
    build(nc, *args, out)
    r = run_bass_kernel_spmd(nc, [{name + "_dram": a for name, a in arrays.items()}], core_ids=[0])
    return r.results[0]["out_dram"]
```

```python
import concourse.bass as bass
from concourse import mybir
from contextlib import ExitStack

B, T, E = 8, 1024, 256
H, D = 8, 128
P = 128
CT = E // P
CHUNK = 256
TPC = CHUNK // P
NC = T // CHUNK
NT = T // P
PAIRS = H // 2
STEPS = NT * H
SCALE = float(D) ** -0.5
EPS = 1e-5
MASKED = 1e30
HUGE = 3e38
T_LAG = 3
PV_LAG = 6
XBUF = 4
LEAD = 6
LAST_IT = STEPS + LEAD
PER = TPC * H


def fillers():
    at = {it: [] for it in range(LAST_IT)}
    for c in range(NC):
        turns = {1: ("FK", c, 0), 6: ("XT", c + 1, 0), 8: ("FV", c, 0), 9: ("KV", c + 1, 0),
                 10: ("Q", c + 1, 0), 11: ("Q", c + 1, 1), 12: ("Q", c + 1, 2), 13: ("WO", c, 0),
                 3: ("Q", c, 3), 15: ("KT", c + 1, 0)}
        for i, u in sorted(turns.items()):
            at[c * PER + i].append(u)
        at[c * PER + PER + 5].append(("WO", c, 1))
    for c in range(NC):
        at[c * PER + 5].append(("FR", c, 0))
    return at


FILL = fillers()
START = [("XT", 0, 0), ("KV", 0, 0), ("KT", 0, 0)] + [("Q", 0, p) for p in range(PAIRS - 1)]
SHARED = NT // 2 * H
G_BANK = {u: k % 3 for k, u in enumerate(START)}
for k, u in enumerate([u for it in range(SHARED) for u in FILL[it]]):
    G_BANK[u] = (k + 1) % 3
G_ORDER = [(0, u) for it in range(LEAD, STEPS) for u in FILL[it]]
for lead in range(LEAD):
    G_ORDER += [(0, u) for u in FILL[STEPS + lead]] + [(1, u) for u in FILL[lead]]
G_FIRST = [(None, u) for u in START] + [(0, u) for lead in range(LEAD) for u in FILL[lead]]


def used_before(order, k):
    bank = G_BANK.get(order[k][1], 0)
    for back in range(1, len(order)):
        if G_BANK.get(order[k - back][1], 0) == bank:
            return k - back, order[k - back]
    return None


def t_banks(s):
    n = s // H + 1
    return [(k, min(4, n - k)) for k in range(0, n, 4)]


T_FIRST = [sum(len(t_banks(r)) for r in range(s)) for s in range(STEPS + 1)]
T_BODY = T_FIRST[STEPS]


def build(nc, x_d, wq_d, wkv_d, wo_d, wr_d, wk_d, wv_d, bq_d, bkv_d, mu_d, pet_d, petok_d, out_d):
    F, R = mybir.dt.float32, mybir.dt.float32r
    ALU, ACT = mybir.AluOpType, mybir.ActivationFunctionType

    x_v = x_d.rearrange("b (c t p) e -> (b c) p t e", t=TPC, p=P)
    out_v = out_d.rearrange("b (n p) e -> (b n) p e", p=P)

    with ExitStack() as ctx:
        def sb(name, shape, dt=F):
            return ctx.enter_context(nc.sbuf_tensor(name, shape, dt))

        def pb(name, shape):
            return ctx.enter_context(nc.psum_tensor(name, shape, F))

        def sem(name):
            return ctx.enter_context(nc.semaphore(name))

        wq = [sb(f"wq{i}", [P, CT, H * D], R) for i in range(2)]
        wkv = [sb(f"wkv{i}", [P, CT, 2 * D], R) for i in range(2)]
        wo = [sb(f"wo{i}", [P, H, E], R) for i in range(2)]
        wr = [sb(f"wr{i}", [P, CT, E], R) for i in range(2)]
        wk = [sb(f"wk{i}", [P, CT, E], R) for i in range(2)]
        wv = [sb(f"wv{i}", [P, CT, E], R) for i in range(2)]
        bq = sb("bq", [P, H])
        mu = sb("mu", [P, 4])
        omu = sb("omu", [P, 4])
        bkv = sb("bkv", [P, 2 * D])
        kpos = sb("kpos", [P, NT, D])
        pet = sb("pet", [P, T])
        mask = sb("mask", [P, T])
        ident = sb("ident", [P, P])
        kt = [sb(f"kt{i}", [P, T], R) for i in range(2)]
        v = [sb(f"v{i}", [P, NT, D], R) for i in range(2)]
        xtok = sb("xtok", [P, NC, TPC, E])
        xn = sb("xn", [P, TPC, E])
        stats = sb("stats", [P, TPC, 6])
        mv = sb("mv", [P, TPC, 2])
        rstd = sb("rstd", [P, TPC])
        vare = sb("vare", [P, TPC])
        half = sb("half", [P, TPC])
        xnt = sb("xnt", [P, 2, CT, CHUNK + 1])
        xt = [sb(f"xt{i}", [P, 2, CT, CHUNK], R) for i in range(2)]
        qt = [sb(f"qt{i}", [P, 2, H, CHUNK], R) for i in range(2)]
        qtmp = sb("qtmp", [P, 2, CHUNK])
        mix = sb("mix", [P, CT, CHUNK])
        mh = [sb(f"mh{i}", [P, CT, CHUNK], R) for i in range(2)]
        ka = sb("ka", [P, CT, CHUNK])
        kh = [sb(f"kh{i}", [P, CT, CHUNK], R) for i in range(2)]
        gate = sb("gate", [P, TPC, E])
        gated = sb("gated", [P, TPC, E])
        X = sb("X", [P, XBUF, T])
        bias = sb("bias", [P, XBUF])
        total = sb("total", [P, XBUF])
        rec = sb("rec", [P, XBUF])
        pt = [sb(f"pt{i}", [P, 2, NT, 2 * P], R) for i in range(2)]
        ot = [sb(f"ot{i}", [P, H, P], R) for i in range(2)]

        pS = [pb(f"pS{i}", [P, 2, 512]) for i in range(2)]
        pT = [pb(f"pT{i}", [P, 512]) for i in range(2)]
        pO = pb("pO", [P, 512])
        pG = pb("pG", [P, 512])

        x_loaded = [sem(f"x_loaded{c}") for c in range(NC)]
        small_loaded = sem("small_loaded")
        wa_loaded = sem("wa_loaded")
        wo_loaded = sem("wo_loaded")
        wa_hi = sem("wa_hi")
        wa_lo = sem("wa_lo")
        wo_hi = sem("wo_hi")
        wo_lo = sem("wo_lo")
        consts = sem("consts")
        kpos_ready = sem("kpos_ready")
        filled = {k: sem(f"filled_{k}") for k in ("XT", "KV", "KT", "Q", "FK", "FR", "FV", "WO")}
        bn_done = sem("bn_done")
        var_ready = sem("var_ready")
        rstd_ready = sem("rstd_ready")
        xn_ready = sem("xn_ready")
        xnt_ready = sem("xnt_ready")
        xnt_kept = sem("xnt_kept")
        xnt_zero = sem("xnt_zero")
        xt_hi = sem("xt_hi")
        xt_ready = sem("xt_ready")
        kv_ready = sem("kv_ready")
        kt_hi = sem("kt_hi")
        kt_ready = sem("kt_ready")
        v_hi = sem("v_hi")
        v_ready = sem("v_ready")
        q_sum = sem("q_sum")
        q_hi = sem("q_hi")
        q_ready = sem("q_ready")
        prev_ready = sem("prev_ready")
        mix_ready = sem("mix_ready")
        mix_hi = sem("mix_hi")
        mix_split = sem("mix_split")
        relu_ready = sem("relu_ready")
        square_ready = sem("square_ready")
        ka_hi = sem("ka_hi")
        ka_split = sem("ka_split")
        tanh_ready = sem("tanh_ready")
        gate_ready = sem("gate_ready")
        gated_ready = sem("gated_ready")
        mixed = sem("mixed")
        out_ready = sem("out_ready")
        stored = [sem(f"stored{c}") for c in range(NC)]
        s_filled = sem("s_filled")
        masked = sem("masked")
        exp_done = sem("exp_done")
        rec_ready = sem("rec_ready")
        normed = sem("normed")
        t_filled = sem("t_filled")
        t_hi = sem("t_hi")
        t_lo = sem("t_lo")
        pv_done = sem("pv_done")
        o_hi = sem("o_hi")
        o_lo = sem("o_lo")
        dve_passed = sem("dve_passed")
        pool_passed = sem("pool_passed")

        stage = X[:, :, :].rearrange("p a n -> p (a n)")
        SIZES = [("wq", CT * H * D), ("wkv", CT * 2 * D), ("wr", CT * E), ("wk", CT * E), ("wv", CT * E)]
        OFF = {}
        off = 0
        for name, n in SIZES:
            OFF[name] = (off, n)
            off += n
        W = {"wq": wq, "wkv": wkv, "wr": wr, "wk": wk, "wv": wv}

        def staged(name):
            a, n = OFF[name]
            return stage[:, a:a + n].rearrange("p (t n) -> p t n", t=CT)

        wo_stage = stage[:, 0:H * E].rearrange("p (t n) -> p t n", t=H)

        def chunk_no(b, c):
            return 0 if b is None else b * NC + c

        def g_bank(*u):
            k = G_BANK.get(u, 0)
            return pS[k - 1][:, 1, :] if k else pG[:, :]

        block = ctx.enter_context(nc.Block())

        @block.sync
        def _(sp):
            sp.dma_start(xtok[:, 0, :, :], x_v[0, :, :, :]).then_inc(x_loaded[0], 16)
            for name, src in (("wkv", wkv_d), ("wq", wq_d), ("wk", wk_d), ("wr", wr_d), ("wv", wv_d)):
                sp.dma_start(staged(name), src.rearrange("(t p) n -> p t n", p=P)).then_inc(wa_loaded, 16)
            sp.wait_ge(wa_lo, len(SIZES))
            sp.dma_start(wo_stage, wo_d.rearrange("(t p) n -> p t n", p=P)).then_inc(wo_loaded, 16)
            for c in range(1, NC):
                sp.dma_start(xtok[:, c, :, :], x_v[c, :, :, :]).then_inc(x_loaded[c], 16)

            def store(b, c, t):
                sp.wait_ge(out_ready, b * NT + c * TPC + t + 1)
                sp.dma_start(out_v[bass.ds(b * NT + c * TPC + t, 1), :, :].rearrange("a p e -> (a p) e"),
                             xtok[:, c, t, :]).then_inc(stored[c], 16)

            with sp.Fori(0, B) as b:
                for c in range(NC):
                    for t in range(TPC):
                        store(b, c, t)
                    sp.wait_ge(stored[c], (b + 1) * (16 * TPC))
                    sp.dma_start(xtok[:, c, :, :],
                                 x_v[bass.ds((b * NC + NC + c) % (B * NC), 1), :, :, :]
                                 .rearrange("a p t e -> (a p) t e")).then_inc(x_loaded[c], 16)
            for c in range(NC):
                sp.wait_ge(stored[c], 16 * TPC * B)
                sp.wait_ge(x_loaded[c], 16 * (B + 1))

        @block.gpsimd
        def _(pool):
            pool.dma_start(bkv[:, :], bkv_d).then_inc(small_loaded, 16)
            pool.dma_start(kpos[:, :, :], petok_d.rearrange("(n p) d -> p n d", p=P)).then_inc(small_loaded, 16)
            pool.dma_start(bq[:, :], bq_d).then_inc(small_loaded, 16)
            pool.dma_start(mu[:, :], mu_d).then_inc(small_loaded, 16)
            pool.dma_start(pet[:, :], pet_d).then_inc(small_loaded, 16)
            nc.gpsimd.memset(ident[:, :], 0.0).then_inc(consts, 1)
            nc.gpsimd.memset(half[:, :], -0.5).then_inc(consts, 1)
            nc.gpsimd.memset(mask[:, :], 0.0).then_inc(consts, 1)
            pool.wait_ge(consts, 3)
            nc.gpsimd.affine_select(out=ident[:, :], in_=ident[:, :], compare_op=ALU.not_equal, fill=1.0,
                                    base=0, pattern=[[-1, P]], channel_multiplier=1).then_inc(consts, 1)
            tri = mask[:, T - P:T]
            nc.gpsimd.affine_select(out=tri, in_=tri, compare_op=ALU.is_ge, fill=MASKED,
                                    base=0, pattern=[[-1, P]], channel_multiplier=1).then_inc(consts, 1)

            def inv_std(n):
                pool.wait_ge(var_ready, n + 1)
                nc.gpsimd.tensor_tensor(rstd[:, :], vare[:, :], half[:, :], ALU.pow).then_inc(rstd_ready, 1)

            def split_xt(n, slot):
                pool.wait_ge(xnt_ready, n + 1)
                nc.gpsimd.tensor_tensor(xt[1][:, slot, :, :], xnt[:, slot, :, 1:CHUNK + 1],
                                        xt[0][:, slot, :, :].bitcast(F), ALU.subtract).then_inc(xt_ready, 1)

            def split_v(n, c):
                pool.wait_ge(v_hi, n + 1)
                tiles = slice(c * TPC, (c + 1) * TPC)
                nc.gpsimd.tensor_tensor(v[1][:, tiles, :], xn[:, :, D:2 * D], v[0][:, tiles, :].bitcast(F),
                                        ALU.subtract).then_inc(v_ready, 1)

            def split_q(n, slot, p):
                pool.wait_ge(q_hi, n * PAIRS + p + 1)
                hs = slice(2 * p, 2 * p + 2)
                nc.gpsimd.tensor_tensor(qt[1][:, slot, hs, :], qtmp[:, :, :], qt[0][:, slot, hs, :].bitcast(F),
                                        ALU.subtract).then_inc(q_ready, 1)

            def split_mix(n, which):
                pool.wait_ge(mix_hi, 2 * n + which + 1)
                nc.gpsimd.tensor_tensor(mh[1][:, :, :], mix[:, :, :], mh[0][:, :, :].bitcast(F),
                                        ALU.subtract).then_inc(mix_split, 1)

            def turn(b, it):
                s = it - 1
                if 0 <= s < STEPS:
                    w = (s // H + 1) * P
                    j = s % XBUF
                    pool.wait_ge(rec_ready, b * STEPS + s + 1)
                    pool.sem_inc(pool_passed, 1)
                    nc.gpsimd.tensor_scalar(X[:, j, 0:w], X[:, j, 0:w], rec[:, j:j + 1], 1.0,
                                            ALU.mult, ALU.mult).then_inc(normed, 1)
                c, i = it // PER, it % PER
                if it < STEPS:
                    if i == 0:
                        inv_std(chunk_no(b, c + 1))
                    if i == 2:
                        split_mix(chunk_no(b, c), 1)
                        pool.wait_ge(ka_hi, b * NC + c + 1)
                        nc.gpsimd.tensor_tensor(kh[1][:, :, :], ka[:, :, :], kh[0][:, :, :].bitcast(F),
                                                ALU.subtract).then_inc(ka_split, 1)
                    if i == 14:
                        split_mix(chunk_no(b, c + 1), 0)
                elif it == STEPS + 4:
                    split_v(chunk_no(b, NC), 0)
                for kind, c, p in FILL[it]:
                    if kind == "XT":
                        split_xt(chunk_no(b, c), c % 2)
                    elif kind == "KV" and c < NC:
                        split_v(chunk_no(b, c), c)
                    elif kind == "Q":
                        split_q(chunk_no(b, c), c % 2, p)
                    elif kind == "FK":
                        pool.wait_ge(relu_ready, b * NC + c + 1)
                        nc.gpsimd.tensor_tensor(ka[:, :, :], ka[:, :, :], ka[:, :, :], ALU.mult
                                                ).then_inc(square_ready, 1)
                    elif kind == "FV":
                        pool.wait_ge(gated_ready, b * NC + c + 1)
                        nc.gpsimd.tensor_tensor(xtok[:, c, :, :], xtok[:, c, :, :], gated[:, :, :],
                                                ALU.add).then_inc(mixed, 1)

            inv_std(0)
            split_xt(0, 0)
            split_v(0, 0)
            for p in range(PAIRS - 1):
                split_q(0, 0, p)
            split_mix(0, 0)
            for it in range(LEAD):
                turn(0, it)
            with pool.Fori(0, B) as b:
                for it in range(LEAD, STEPS):
                    turn(b, it)
                for it in range(LEAD):
                    turn(b, STEPS + it)
                    turn(b + 1, it)

        @block.scalar
        def _(act):
            for n, (name, _) in enumerate((("wkv", 0), ("wq", 0), ("wk", 0), ("wr", 0), ("wv", 0))):
                if n == 0:
                    act.wait_ge(wa_loaded, 16 * len(SIZES))
                nc.scalar.copy(W[name][0][:, :, :], staged(name)).then_inc(wa_hi, 1)

            def xt_out(b, c):
                n = chunk_no(b, c)
                slot = c % 2
                act.wait_ge(filled["XT"], n + 1)
                g = g_bank("XT", c, 0).rearrange("p (t n) -> p t n", t=CT)
                if c % NC:
                    nc.scalar.copy(xnt[:, slot, :, 0:1], xnt[:, 1 - slot, :, CHUNK:CHUNK + 1]
                                   ).then_inc(xnt_kept, 1)
                nc.scalar.copy(xt[0][:, slot, :, :], g).then_inc(xt_hi, 1)
                nc.scalar.copy(xnt[:, slot, :, 1:CHUNK + 1], g).then_inc(xnt_ready, 1)

            def kt_out(b, c):
                act.wait_ge(filled["KT"], chunk_no(b, c) + 1)
                k0 = (c % NC) * CHUNK
                nc.scalar.activation(kt[0][:, k0:k0 + CHUNK], g_bank("KT", c, 0)[:, 0:CHUNK], ACT.Copy, scale=-1.0
                                     ).then_inc(kt_hi, 1)

            def v_out(b, c):
                act.wait_ge(kv_ready, 2 * chunk_no(b, c) + 2)
                tiles = slice((c % NC) * TPC, (c % NC + 1) * TPC)
                nc.scalar.copy(v[0][:, tiles, :], xn[:, :, D:2 * D]).then_inc(v_hi, 1)

            def q_out(b, c, p):
                act.wait_ge(q_sum, (chunk_no(b, c) * PAIRS + p) * 2 + 2)
                nc.scalar.copy(qt[0][:, c % 2, 2 * p:2 * p + 2, :], qtmp[:, :, :]).then_inc(q_hi, 1)

            def mix_out(n, which):
                act.wait_ge(mix_ready, (2 * n + which + 1) * CT)
                nc.scalar.copy(mh[0][:, :, :], mix[:, :, :]).then_inc(mix_hi, 1)

            def turn(b, it):
                first = it - PV_LAG
                if 0 <= first < STEPS and first % 2 == 0:
                    pair = first // 2
                    act.wait_ge(pv_done, b * (STEPS // 2) + pair + 1)
                    h = first % H
                    if h == 0 and not (isinstance(b, int) and pair == 0):
                        act.wait_ge(filled["WO"], b * NT + first // H)
                    nc.scalar.copy(ot[0][:, h:h + 2, :],
                                   pO[:, 0:2 * P].rearrange("p (h q) -> p h q", h=2)).then_inc(o_hi, 1)
                s = it - T_LAG
                if 0 <= s < STEPS:
                    half_q = slice((s % 2) * P, (s % 2 + 1) * P)
                    for m, (k, nk) in enumerate(t_banks(s)):
                        u = T_FIRST[s] + m
                        act.wait_ge(t_filled, b * T_BODY + u + 1)
                        nc.scalar.copy(pt[0][:, (s // 2) % 2, k:k + nk, half_q],
                                       pT[u % 2][:, 0:nk * P].rearrange("p (k q) -> p k q", k=nk)
                                       ).then_inc(t_hi, 1)
                s = it - 1
                if 0 <= s < STEPS:
                    w = (s // H + 1) * P
                    j = s % XBUF
                    act.wait_ge(masked, b * STEPS + s + 1)
                    nc.scalar.activation(X[:, j, 0:w], X[:, j, 0:w], ACT.Exp, bias=bias[:, j:j + 1],
                                         scale=-1.0, accum_out=total[:, j:j + 1]).then_inc(exp_done, 1)
                for kind, c, p in FILL[it]:
                    if kind == "XT":
                        xt_out(b, c)
                    elif kind == "KT":
                        if c == NC:
                            act.wait_ge(s_filled, (b + 1) * STEPS)
                        kt_out(b, c)
                    elif kind == "KV" and c < NC:
                        v_out(b, c)
                    elif kind == "FK":
                        act.wait_ge(filled["FK"], b * NC + c + 1)
                        nc.scalar.activation(ka[:, :, :], g_bank(kind, c, p).rearrange("p (t n) -> p t n", t=CT),
                                             ACT.Relu).then_inc(relu_ready, 1)
                    elif kind == "FR":
                        act.wait_ge(filled["FR"], b * NC + c + 1)
                        nc.scalar.activation(gate[:, :, :], g_bank(kind, c, p).rearrange("p (t n) -> p t n", t=TPC),
                                             ACT.Tanh, scale=0.5).then_inc(tanh_ready, 1)
                    elif kind == "Q":
                        q_out(b, c, p)
                c, i = it // PER, it % PER
                if it < STEPS:
                    if i == 2:
                        mix_out(chunk_no(b, c), 1)
                        act.wait_ge(square_ready, b * NC + c + 1)
                        nc.scalar.copy(kh[0][:, :, :], ka[:, :, :]).then_inc(ka_hi, 1)
                    if i == 14:
                        act.wait_ge(filled["FR"], b * NC + c + 1)
                        mix_out(chunk_no(b, c + 1), 0)
                elif it == STEPS + 4:
                    act.wait_ge(pv_done, (b + 1) * (STEPS // 2))
                    v_out(b, NC)

            xt_out(None, 0)
            kt_out(None, 0)
            v_out(None, 0)
            for p in range(PAIRS - 1):
                q_out(None, 0, p)
            mix_out(0, 0)
            act.wait_ge(wo_loaded, 16)
            nc.scalar.copy(wo[0][:, :, :], wo_stage).then_inc(wo_hi, 1)
            for it in range(LEAD):
                turn(0, it)
            with act.Fori(0, B) as b:
                for it in range(LEAD, STEPS):
                    turn(b, it)
                for it in range(LEAD):
                    turn(b, STEPS + it)
                    turn(b + 1, it)

        @block.vector
        def _(dve):
            def norm_stats(n, slot, b):
                dve.wait_ge(x_loaded[slot], 16 if b is None else 16 * ((b + 1) if slot else (b + 2)))
                for t in range(TPC):
                    nc.vector.bn_stats(stats[:, t, :], xtok[:, slot, t, :]).then_inc(bn_done, 1)
                dve.wait_ge(bn_done, n * 2 * TPC + TPC)
                dve.sem_inc(dve_passed, 1)
                for t in range(TPC):
                    nc.vector.bn_aggr(mv[:, t, :], stats[:, t, :]).then_inc(bn_done, 1)
                dve.wait_ge(bn_done, n * 2 * TPC + 2 * TPC)
                nc.vector.tensor_scalar_add(vare[:, :], mv[:, :, 1], EPS).then_inc(var_ready, 1)

            def norm_apply(n, slot):
                dve.wait_ge(rstd_ready, n + 1)
                for t in range(TPC):
                    nc.vector.tensor_scalar(xn[:, t, :], xtok[:, slot, t, :], mv[:, t, 0:1], rstd[:, t:t + 1],
                                            ALU.subtract, ALU.mult).then_inc(xn_ready, 1)

            def kv_out(b, c):
                n = chunk_no(b, c)
                dve.wait_ge(filled["KV"], chunk_no(b, c) + 1)
                g = g_bank("KV", c, 0).rearrange("p (t n) -> p t n", t=TPC)
                tiles = slice((c % NC) * TPC, (c % NC + 1) * TPC)
                nc.vector.tensor_tensor(xn[:, :, 0:D], g[:, :, 0:D], kpos[:, tiles, :], ALU.add
                                        ).then_inc(kv_ready, 1)
                nc.vector.tensor_tensor(xn[:, :, D:2 * D], g[:, :, D:2 * D],
                                        bkv[:, D:2 * D].rearrange("p (a n) -> p a n", a=1).broadcast_to((P, TPC, D)),
                                        ALU.add).then_inc(kv_ready, 1)

            def kt_out(b, c):
                dve.wait_ge(kt_hi, chunk_no(b, c) + 1)
                k0 = (c % NC) * CHUNK
                nc.vector.scalar_tensor_tensor(kt[1][:, k0:k0 + CHUNK], g_bank("KT", c, 0)[:, 0:CHUNK], -1.0,
                                               kt[0][:, k0:k0 + CHUNK].bitcast(F), ALU.mult, ALU.subtract
                                               ).then_inc(kt_ready, 1)

            def q_out(b, c, p):
                n = chunk_no(b, c)
                dve.wait_ge(filled["Q"], chunk_no(b, c) * PAIRS + p + 1)
                if b is not None or p:
                    dve.wait_ge(q_ready, n * PAIRS + p)
                t0 = (c % NC) * CHUNK
                for i in range(2):
                    h = 2 * p + i
                    nc.vector.scalar_tensor_tensor(qtmp[:, i, :], g_bank("Q", c, p)[:, i * CHUNK:(i + 1) * CHUNK], bq[:, h:h + 1],
                                                   pet[:, t0:t0 + CHUNK], ALU.add, ALU.add).then_inc(q_sum, 1)

            def token_mix(n, slot, which):
                n = 2 * n + which
                x_now = xnt[:, slot, :, 1:CHUNK + 1]
                x_before = xnt[:, slot, :, 0:CHUNK]
                for t in range(CT):
                    m = (1 - which) * CT + t
                    nc.vector.tensor_scalar(mix[:, t, :], x_before[:, t, :], omu[:, m:m + 1], None, ALU.mult
                                            ).then_inc(prev_ready, 1)
                dve.wait_ge(prev_ready, n * CT + CT)
                for t in range(CT):
                    m = (1 - which) * CT + t
                    nc.vector.scalar_tensor_tensor(mix[:, t, :], x_now[:, t, :], mu[:, m:m + 1], mix[:, t, :],
                                                   ALU.mult, ALU.add).then_inc(mix_ready, 1)

            norm_stats(0, 0, None)
            dve.wait_ge(small_loaded, 80)
            nc.vector.tensor_scalar(omu[:, :], mu[:, :], -1.0, 1.0, ALU.mult, ALU.add).then_inc(kpos_ready, 1)
            nc.vector.tensor_tensor(kpos[:, :, :], kpos[:, :, :],
                                    bkv[:, 0:D].rearrange("p (a n) -> p a n", a=1).broadcast_to((P, NT, D)),
                                    ALU.add).then_inc(kpos_ready, 1)
            nc.vector.memset(xnt[:, 0, :, 0:1], 0.0).then_inc(xnt_zero, 1)
            norm_apply(0, 0)
            for n, name in enumerate(("wkv", "wq", "wk", "wr", "wv")):
                dve.wait_ge(wa_hi, n + 1)
                nc.vector.tensor_tensor(W[name][1][:, :, :], staged(name), W[name][0][:, :, :].bitcast(F),
                                        ALU.subtract).then_inc(wa_lo, 1)
            dve.wait_ge(kpos_ready, 2)
            kv_out(None, 0)
            kt_out(None, 0)
            for p in range(PAIRS - 1):
                q_out(None, 0, p)
            dve.wait_ge(xnt_ready, 1)
            dve.wait_ge(xnt_zero, 1)
            token_mix(0, 0, 0)
            dve.wait_ge(wo_hi, 1)
            nc.vector.tensor_tensor(wo[1][:, :, :], wo_stage, wo[0][:, :, :].bitcast(F), ALU.subtract
                                    ).then_inc(wo_lo, 1)
            dve.wait_ge(wo_lo, 1)
            dve.wait_ge(consts, 5)

            def turn(b, it):
                first_row = isinstance(b, int)
                first = it - PV_LAG
                if 0 <= first < STEPS and first % 2 == 0:
                    pair = first // 2
                    dve.wait_ge(o_hi, b * (STEPS // 2) + pair + 1)
                    h = first % H
                    nc.vector.tensor_tensor(ot[1][:, h:h + 2, :],
                                            pO[:, 0:2 * P].rearrange("p (h q) -> p h q", h=2),
                                            ot[0][:, h:h + 2, :].bitcast(F), ALU.subtract).then_inc(o_lo, 1)
                s = it - T_LAG
                if 0 <= s < STEPS:
                    half_q = slice((s % 2) * P, (s % 2 + 1) * P)
                    for m, (k, nk) in enumerate(t_banks(s)):
                        u = T_FIRST[s] + m
                        dve.wait_ge(t_hi, b * T_BODY + u + 1)
                        nc.vector.tensor_tensor(pt[1][:, (s // 2) % 2, k:k + nk, half_q],
                                                pT[u % 2][:, 0:nk * P].rearrange("p (k q) -> p k q", k=nk),
                                                pt[0][:, (s // 2) % 2, k:k + nk, half_q].bitcast(F),
                                                ALU.subtract).then_inc(t_lo, 1)
                for kind, c, p in FILL[it]:
                    n = chunk_no(b, c)
                    if kind == "XT":
                        if c == NC:
                            nc.vector.memset(xnt[:, 0, :, 0:1], 0.0).then_inc(xnt_zero, 1)
                    elif kind == "KV":
                        kv_out(b, c)
                    elif kind == "KT":
                        kt_out(b, c)
                    elif kind == "Q":
                        q_out(b, c, p)
                    elif kind == "FR":
                        dve.wait_ge(tanh_ready, n + 1)
                        nc.vector.tensor_scalar(gate[:, :, :], gate[:, :, :], 0.5, 0.5, ALU.mult, ALU.add
                                                ).then_inc(gate_ready, 1)
                    elif kind == "FV":
                        dve.wait_ge(gate_ready, n + 1)
                        dve.wait_ge(filled["FV"], n + 1)
                        nc.vector.tensor_tensor(gated[:, :, :], g_bank(kind, c, p).rearrange("p (t n) -> p t n", t=TPC),
                                                gate[:, :, :], ALU.mult).then_inc(gated_ready, 1)
                    elif kind == "WO":
                        dve.wait_ge(mixed, n + 1)
                        dve.wait_ge(filled["WO"], b * NT + c * TPC + p + 1)
                        nc.vector.tensor_tensor(xtok[:, c, p, :], g_bank(kind, c, p)[:, 0:E], xtok[:, c, p, :], ALU.add
                                                ).then_inc(out_ready, 1)
                c, i = it // PER, it % PER
                if it < STEPS:
                    n = chunk_no(b, c)
                    if i == 0:
                        norm_stats(chunk_no(b, c + 1), (c + 1) % NC, b)
                    elif i == 1:
                        dve.wait_ge(mix_split, 2 * n + 1)
                        token_mix(n, c % 2, 1)
                    elif i == 5:
                        dve.wait_ge(v_ready, n + 1)
                        dve.wait_ge(filled["KT"], n + 1)
                        norm_apply(chunk_no(b, c + 1), (c + 1) % NC)
                    elif i == 13:
                        n = chunk_no(b, c + 1)
                        dve.wait_ge(mix_split, 2 * n)
                        dve.wait_ge(xnt_ready, n + 1)
                        if c == NC - 1:
                            dve.wait_ge(xnt_zero, b + 2)
                        token_mix(n, (c + 1) % 2, 0)
                s = it
                if s < STEPS:
                    qi = s // H
                    w = (qi + 1) * P
                    j = s % XBUF
                    if qi < 4:
                        scores = pS[s % 2][:, 0, 0:w]
                        m = mask[:, T - w:T]
                        o = X[:, j, 0:w]
                    else:
                        scores = pS[s % 2][:, :, 0:w // 2]
                        m = mask[:, T - w:T].rearrange("p (a n) -> p a n", a=2)
                        o = X[:, j, 0:w].rearrange("p (a n) -> p a n", a=2)
                    if s >= XBUF:
                        dve.wait_ge(t_filled, b * T_BODY + T_FIRST[s - XBUF + 1])
                    elif not first_row:
                        dve.wait_ge(t_filled, (b - 1) * T_BODY + T_FIRST[STEPS + s - XBUF + 1])
                    dve.wait_ge(s_filled, b * STEPS + s + 1)
                    dve.sem_inc(dve_passed, 1)
                    nc.vector.tensor_tensor_reduce(out=o, in0=scores, in1=m, scale=SCALE, scalar=HUGE,
                                                   op0=ALU.add, op1=ALU.min,
                                                   accum_out=bias[:, j:j + 1]).then_inc(masked, 1)
                s = it - 1
                if 0 <= s < STEPS:
                    j = s % XBUF
                    dve.wait_ge(exp_done, b * STEPS + s + 1)
                    nc.vector.reciprocal(rec[:, j:j + 1], total[:, j:j + 1]).then_inc(rec_ready, 1)

            for it in range(LEAD):
                turn(0, it)
            with dve.Fori(0, B) as b:
                for it in range(LEAD, STEPS):
                    turn(b, it)
                for it in range(LEAD):
                    turn(b, STEPS + it)
                    turn(b + 1, it)

        @block.tensor
        def _(pe):
            PASSES = ((0, 0), (0, 1), (1, 0))

            def product(out, terms, start=True):
                n = len(terms) * len(PASSES)
                k = 0
                for a, m in terms:
                    for i, j in PASSES:
                        last = nc.tensor.matmul(out, a[i], m[j], start=start and k == 0, stop=k == n - 1)
                        k += 1
                return last

            def wait_emptied(b, u):
                kind, c, p = u
                n = chunk_no(b, c)
                if kind == "XT":
                    pe.wait_ge(xnt_ready, n + 1)
                elif kind == "KV":
                    pe.wait_ge(kv_ready, 2 * n + 2)
                elif kind == "KT":
                    pe.wait_ge(kt_ready, n + 1)
                elif kind == "Q":
                    pe.wait_ge(q_sum, (n * PAIRS + p) * 2 + 2)
                elif kind == "FK":
                    pe.wait_ge(relu_ready, n + 1)
                elif kind == "FR":
                    pe.wait_ge(tanh_ready, n + 1)
                elif kind == "FV":
                    pe.wait_ge(gated_ready, n + 1)
                else:
                    pe.wait_ge(out_ready, b * NT + c * TPC + p + 1)

            def fill(b, u, row, place):
                kind, c, p = u
                out = g_bank(kind, c, p)
                if row is None:
                    k = [x for _, x in G_FIRST].index(u)
                    found = used_before(G_FIRST, k)
                    if found and found[0] >= 0:
                        wait_emptied(*found[1])
                else:
                    found, (rows, before) = used_before(G_ORDER, G_ORDER.index((place, u)))
                    if found >= 0 or rows:
                        wait_emptied(row + rows - (found < 0), before)
                n = chunk_no(b, c)
                slot = c % 2
                if kind == "XT":
                    pe.wait_ge(xn_ready, n * TPC + TPC)
                    for ct in range(CT):
                        for t in range(TPC):
                            o = ct * CHUNK + t * P
                            last = nc.tensor.transpose(out[:, o:o + P], xn[:, t, ct * P:(ct + 1) * P], ident[:, :])
                elif kind == "KV":
                    pe.wait_ge(xt_ready, n + 1)
                    for t in range(TPC):
                        last = product(out[:, t * 2 * D:(t + 1) * 2 * D],
                                       [([x[:, slot, ct, t * P:(t + 1) * P] for x in xt],
                                         [w[:, ct, :] for w in wkv]) for ct in range(CT)])
                elif kind == "KT":
                    pe.wait_ge(kv_ready, 2 * n + 2)
                    for t in range(TPC):
                        last = nc.tensor.transpose(out[:, t * P:(t + 1) * P], xn[:, t, 0:D], ident[:, :])
                elif kind == "Q":
                    for i in range(2):
                        h = 2 * p + i
                        last = product(out[:, i * CHUNK:(i + 1) * CHUNK],
                                       [([w[:, ct, h * D:(h + 1) * D] for w in wq],
                                         [x[:, slot, ct, :] for x in xt]) for ct in range(CT)])
                elif kind == "FK":
                    pe.wait_ge(mix_split, (b * NC + c) * 2 + 1)
                    for j in range(CT):
                        last = product(out[:, j * CHUNK:(j + 1) * CHUNK],
                                       [([w[:, ct, j * P:(j + 1) * P] for w in wk],
                                         [m[:, ct, :] for m in mh]) for ct in range(CT)])
                elif kind == "FR":
                    pe.wait_ge(mix_split, (b * NC + c) * 2 + 2)
                    for t in range(TPC):
                        last = product(out[:, t * E:(t + 1) * E],
                                       [([m[:, ct, t * P:(t + 1) * P] for m in mh],
                                         [w[:, ct, :] for w in wr]) for ct in range(CT)])
                elif kind == "FV":
                    pe.wait_ge(ka_split, b * NC + c + 1)
                    for t in range(TPC):
                        last = product(out[:, t * E:(t + 1) * E],
                                       [([m[:, ct, t * P:(t + 1) * P] for m in kh],
                                         [w[:, ct, :] for w in wv]) for ct in range(CT)])
                elif kind == "WO":
                    pe.wait_ge(o_lo, (b * NT + c * TPC + p + 1) * PAIRS)
                    last = product(out[:, 0:E], [([o[:, h, :] for o in ot], [w[:, h, :] for w in wo])
                                                for h in range(H)])
                last.then_inc(filled[kind], 1)

            def turn(b, it, row=None, place=0):
                first_row = isinstance(b, int)
                first = it - PV_LAG
                if 0 <= first < STEPS and first % 2 == 0:
                    pair = first // 2
                    nk = first // H + 1
                    if first % PER == 0:
                        pe.wait_ge(v_ready, b * NC + first // PER + 1)
                    if pair or not first_row:
                        pe.wait_ge(o_lo, b * (STEPS // 2) + pair)
                    pe.wait_ge(t_lo, b * T_BODY + T_FIRST[first + 2])
                    last = product(pO[:, 0:2 * P],
                                   [([x[:, k, :] for x in v], [x[:, pair % 2, k, :] for x in pt])
                                    for k in range(nk)])
                    last.then_inc(pv_done, 1)
                s = it - T_LAG
                if 0 <= s < STEPS:
                    pe.wait_ge(normed, b * STEPS + s + 1)
                    for m, (k, nk) in enumerate(t_banks(s)):
                        u = T_FIRST[s] + m
                        if u >= 2 or not first_row:
                            pe.wait_ge(t_lo, b * T_BODY + u - 1)
                        for i in range(nk):
                            last = nc.tensor.transpose(pT[u % 2][:, i * P:(i + 1) * P],
                                                       X[:, s % XBUF, (k + i) * P:(k + i + 1) * P],
                                                       ident[:, :])
                        last.then_inc(t_filled, 1)
                for u in FILL[it]:
                    fill(b, u, row, place)
                s = it
                if s < STEPS:
                    qi, h = s // H, s % H
                    c, t = qi // TPC, qi % TPC
                    w = (qi + 1) * P
                    n = chunk_no(b, c)
                    if s % PER == 0:
                        pe.wait_ge(kt_ready, n + 1)
                    if t == 0 and h % 2 == 0:
                        pe.wait_ge(q_ready, n * PAIRS + h // 2 + 1)
                    if s >= 2 or not first_row:
                        pe.wait_ge(masked, b * STEPS + s - 1)
                    if SHARED <= s < SHARED + 2:
                        wait_emptied(b, [u for it in range(SHARED) for u in FILL[it]
                                         if G_BANK[u] == s - SHARED + 1][-1])
                    halves = 1 if qi < 4 else 2
                    wn = w // halves
                    for a in range(halves):
                        last = product(pS[s % 2][:, a, 0:wn],
                                       [([q[:, c % 2, h, t * P:(t + 1) * P] for q in qt],
                                         [k[:, a * wn:(a + 1) * wn] for k in kt])])
                    last.then_inc(s_filled, 1)

            pe.wait_ge(consts, 5)
            fill(None, START[0], None, 0)
            pe.wait_ge(wa_lo, len(SIZES))
            for u in START[1:]:
                fill(None, u, None, 0)
            for it in range(LEAD):
                turn(0, it)
            pe.wait_ge(wo_lo, 1)
            with pe.Fori(0, B) as b:
                for it in range(LEAD, STEPS):
                    turn(b, it, b, 0)
                for it in range(LEAD):
                    turn(b, STEPS + it, b, 0)
                    turn(b + 1, it, b, 1)


def _positions():
    import numpy as np
    pos = np.arange(T, dtype=np.float32)[:, None]
    inv = np.exp(np.float32(-np.log(10000.0)) * np.arange(0, D, 2, dtype=np.float32) / np.float32(D))
    ang = (pos * inv.astype(np.float32)[None, :]).astype(np.float32)
    pe = np.zeros((T, D), np.float32)
    pe[:, 0::2] = np.sin(ang)
    pe[:, 1::2] = np.cos(ang)
    return pe


def kernel(L0_attn_x, L0_attn_Wq, L0_attn_bq, L0_attn_Wkv, L0_attn_bkv, L0_attn_Wo, L0_ffn_W_r, L0_ffn_W_k,
           L0_ffn_W_v, L0_ffn_mu_r, L0_ffn_mu_k):
    import numpy as np
    import concourse.bacc as bacc
    from concourse.bass_utils import run_bass_kernel_spmd

    pe = _positions()
    arrays = {
        "x": np.asarray(L0_attn_x),
        "wq": np.asarray(L0_attn_Wq),
        "wkv": np.asarray(L0_attn_Wkv),
        "wo": np.asarray(L0_attn_Wo),
        "wr": np.asarray(L0_ffn_W_r).T,
        "wk": np.asarray(L0_ffn_W_k).T,
        "wv": np.asarray(L0_ffn_W_v).T,
        "bq": np.asarray(L0_attn_bq).reshape(H, D).T,
        "bkv": np.tile(np.asarray(L0_attn_bkv)[None, :], (P, 1)),
        "mu": np.concatenate([np.asarray(L0_ffn_mu_r).reshape(CT, P), np.asarray(L0_ffn_mu_k).reshape(CT, P)]).T,
        "pet": pe.T,
        "petok": pe,
    }
    arrays = {name: np.ascontiguousarray(a) for name, a in arrays.items()}
    nc = bacc.Bacc("TRN2", target_bir_lowering=False, num_devices=1)
    args = [nc.dram_tensor(name + "_dram", a.shape, mybir.dt.from_np(a.dtype), kind="ExternalInput").ap()
            for name, a in arrays.items()]
    out = nc.dram_tensor("out_dram", (B, T, E), mybir.dt.float32, kind="ExternalOutput").ap()
    build(nc, *args, out)
    r = run_bass_kernel_spmd(nc, [{name + "_dram": a for name, a in arrays.items()}], core_ids=[0])
    return r.results[0]["out_dram"]
```

```python
import concourse.bass as bass
from concourse import mybir
from contextlib import ExitStack

B, T, E = 8, 1024, 256
H, D = 8, 128
P = 128
CT = E // P
CHUNK = 256
TPC = CHUNK // P
NC = T // CHUNK
NT = T // P
PAIRS = H // 2
STEPS = NT * H
SCALE = float(D) ** -0.5
EPS = 1e-5
MASKED = 1e30
HUGE = 3e38
T_LAG = 3
PV_LAG = 6
XBUF = 4
MIX_AT = 12
LEAD = 7
LAST_IT = STEPS + LEAD
PER = TPC * H


def fillers():
    at = {it: [] for it in range(LAST_IT)}
    for c in range(NC):
        turns = {2: ("FK", c, 0), 4: ("Q", c, 3), 7: ("XT", c + 1, 0), 8: ("FV", c, 0),
                 9: ("KV", c + 1, 0), 10: ("Q", c + 1, 0), 11: ("KT", c + 1, 0), 12: ("Q", c + 1, 1),
                 13: ("WO", c, 0), 14: ("Q", c + 1, 2)}
        if c == NC - 1:
            turns = {2: ("FK", c, 0), 4: ("Q", c, 3), 7: ("XT", c + 1, 0), 8: ("FV", c, 0),
                     9: ("KV", c + 1, 0), 11: ("Q", c + 1, 0), 12: ("Q", c + 1, 1), 13: ("WO", c, 0),
                     14: ("Q", c + 1, 2), 15: ("KT", c + 1, 0)}
        for i, u in sorted(turns.items()):
            at[c * PER + i].append(u)
        at[c * PER + PER + 5].append(("WO", c, 1))
    for c in range(NC):
        at[c * PER + 6].append(("FR", c, 0))
    return at


FILL = fillers()
START = [("XT", 0, 0), ("KV", 0, 0), ("KT", 0, 0)] + [("Q", 0, p) for p in range(PAIRS - 1)]
SHARED = NT // 2 * H
G_BANK = {u: k % 3 for k, u in enumerate(START)}
for k, u in enumerate([u for it in range(SHARED) for u in FILL[it]]):
    G_BANK[u] = (k + 1) % 3
G_ORDER = [(0, u) for it in range(LEAD, STEPS) for u in FILL[it]]
for lead in range(LEAD):
    G_ORDER += [(0, u) for u in FILL[STEPS + lead]] + [(1, u) for u in FILL[lead]]
G_FIRST = [(None, u) for u in START] + [(0, u) for lead in range(LEAD) for u in FILL[lead]]


def used_before(order, k):
    bank = G_BANK.get(order[k][1], 0)
    for back in range(1, len(order)):
        if G_BANK.get(order[k - back][1], 0) == bank:
            return k - back, order[k - back]
    return None


def t_banks(s):
    n = s // H + 1
    return [(k, min(4, n - k)) for k in range(0, n, 4)]


T_FIRST = [sum(len(t_banks(r)) for r in range(s)) for s in range(STEPS + 1)]
T_BODY = T_FIRST[STEPS]


def build(nc, x_d, wq_d, wkv_d, wo_d, wr_d, wk_d, wv_d, bq_d, bkv_d, mu_d, pet_d, petok_d, out_d):
    F, R = mybir.dt.float32, mybir.dt.float32r
    ALU, ACT = mybir.AluOpType, mybir.ActivationFunctionType

    x_v = x_d.rearrange("b (c t p) e -> (b c) p t e", t=TPC, p=P)
    out_v = out_d.rearrange("b (n p) e -> (b n) p e", p=P)

    with ExitStack() as ctx:
        def sb(name, shape, dt=F):
            return ctx.enter_context(nc.sbuf_tensor(name, shape, dt))

        def pb(name, shape):
            return ctx.enter_context(nc.psum_tensor(name, shape, F))

        def sem(name):
            return ctx.enter_context(nc.semaphore(name))

        wq = [sb(f"wq{i}", [P, CT, H * D], R) for i in range(2)]
        wkv = [sb(f"wkv{i}", [P, CT, 2 * D], R) for i in range(2)]
        wo = [sb(f"wo{i}", [P, H, E], R) for i in range(2)]
        wr = [sb(f"wr{i}", [P, CT, E], R) for i in range(2)]
        wk = [sb(f"wk{i}", [P, CT, E], R) for i in range(2)]
        wv = [sb(f"wv{i}", [P, CT, E], R) for i in range(2)]
        bq = sb("bq", [P, H])
        mu = sb("mu", [P, 4])
        omu = sb("omu", [P, 4])
        bkv = sb("bkv", [P, 2 * D])
        kpos = sb("kpos", [P, NT, D])
        pet = sb("pet", [P, T])
        mask = sb("mask", [P, T])
        ident = sb("ident", [P, P])
        kt = [sb(f"kt{i}", [P, T], R) for i in range(2)]
        v = [sb(f"v{i}", [P, NT, D], R) for i in range(2)]
        xtok = sb("xtok", [P, NC, TPC, E])
        xn = sb("xn", [P, TPC, E])
        stats = sb("stats", [P, TPC, 6])
        mv = sb("mv", [P, TPC, 2])
        rstd = sb("rstd", [P, TPC])
        vare = sb("vare", [P, TPC])
        half = sb("half", [P, TPC])
        xnt = sb("xnt", [P, 2, CT, CHUNK + 1])
        xt = [sb(f"xt{i}", [P, 2, CT, CHUNK], R) for i in range(2)]
        qt = [sb(f"qt{i}", [P, 2, H, CHUNK], R) for i in range(2)]
        qtmp = sb("qtmp", [P, 2, 2, CHUNK])
        mix = sb("mix", [P, CT, CHUNK])
        mh = [sb(f"mh{i}", [P, CT, CHUNK], R) for i in range(2)]
        ka = sb("ka", [P, CT, CHUNK])
        kh = [sb(f"kh{i}", [P, CT, CHUNK], R) for i in range(2)]
        gate = sb("gate", [P, TPC, E])
        X = sb("X", [P, XBUF, T])
        bias = sb("bias", [P, XBUF])
        total = sb("total", [P, XBUF])
        rec = sb("rec", [P, XBUF])
        pt = [sb(f"pt{i}", [P, 2, NT, 2 * P], R) for i in range(2)]
        ot = [sb(f"ot{i}", [P, H, P], R) for i in range(2)]

        pS = [pb(f"pS{i}", [P, 2, 512]) for i in range(2)]
        pT = [pb(f"pT{i}", [P, 512]) for i in range(2)]
        pO = pb("pO", [P, 512])
        pG = pb("pG", [P, 512])

        x_loaded = [sem(f"x_loaded{c}") for c in range(NC)]
        mu_loaded = sem("mu_loaded")
        k_terms_loaded = sem("k_terms_loaded")
        q_terms_loaded = sem("q_terms_loaded")
        omu_ready = sem("omu_ready")
        NAMES = ("wkv", "wq0", "wq1", "wk", "wr", "wv", "wo0", "wo1")
        w_loaded = {name: sem(f"{name}_loaded") for name in NAMES}
        w_hi = {name: sem(f"{name}_hi") for name in NAMES}
        w_lo = {name: sem(f"{name}_lo") for name in NAMES}
        consts = sem("consts")
        kpos_ready = sem("kpos_ready")
        filled = {k: sem(f"filled_{k}") for k in ("XT", "KV", "KT", "Q", "FK", "FR", "FV", "WO")}
        bn_done = sem("bn_done")
        var_ready = sem("var_ready")
        rstd_ready = sem("rstd_ready")
        xn_ready = sem("xn_ready")
        xnt_ready = sem("xnt_ready")
        xnt_zero = sem("xnt_zero")
        xt_ready = sem("xt_ready")
        kv_ready = sem("kv_ready")
        kt_hi = sem("kt_hi")
        kt_ready = sem("kt_ready")
        v_hi = sem("v_hi")
        v_ready = sem("v_ready")
        q_sum = sem("q_sum")
        q_hi = sem("q_hi")
        q_ready = sem("q_ready")
        prev_ready = sem("prev_ready")
        mix_ready = sem("mix_ready")
        mix_hi = sem("mix_hi")
        mix_split = sem("mix_split")
        relu_ready = sem("relu_ready")
        square_ready = sem("square_ready")
        ka_hi = sem("ka_hi")
        ka_split = sem("ka_split")
        tanh_ready = sem("tanh_ready")
        gated_ready = sem("gated_ready")
        mixed = sem("mixed")
        out_ready = sem("out_ready")
        stored = [sem(f"stored{c}") for c in range(NC)]
        s_filled = sem("s_filled")
        masked = sem("masked")
        exp_done = sem("exp_done")
        rec_ready = sem("rec_ready")
        normed = sem("normed")
        t_filled = sem("t_filled")
        t_hi = sem("t_hi")
        t_lo = sem("t_lo")
        pv_done = sem("pv_done")
        o_hi = sem("o_hi")
        o_lo = sem("o_lo")
        dve_passed = sem("dve_passed")
        pool_passed = sem("pool_passed")

        STAGE = {"wq0": X[:, 0:CT, 0:H * D // 2],
                 "wq1": X[:, 0:CT, H * D // 2:H * D],
                 "wkv": X[:, 2, 0:CT * 2 * D].rearrange("p (t n) -> p t n", t=CT),
                 "wk": X[:, 3, 0:CT * E].rearrange("p (t n) -> p t n", t=CT),
                 "wr": X[:, 2:2 + CT, T - E:T],
                 "wv": gate[:, :, :],
                 "wo0": X[:, 0:H // 2, E:2 * E],
                 "wo1": X[:, 0:H // 2, 2 * E:3 * E]}
        W = {"wq0": [w[:, :, 0:H * D // 2] for w in wq], "wq1": [w[:, :, H * D // 2:H * D] for w in wq],
             "wkv": wkv, "wk": wk, "wr": wr, "wv": wv,
             "wo0": [w[:, 0:H // 2, :] for w in wo], "wo1": [w[:, H // 2:H, :] for w in wo]}
        LATE = {1: ("wr", slice(0, CT)), 2: ("wv", slice(0, CT)),
                3: ("wo0", slice(0, 2)), 4: ("wo0", slice(2, 4)), 5: ("wo1", slice(0, 2)), 6: ("wo1", slice(2, 4))}

        def chunk_no(b, c):
            return 0 if b is None else b * NC + c

        def g_bank(*u):
            k = G_BANK.get(u, 0)
            return pS[k - 1][:, 1, :] if k else pG[:, :]

        block = ctx.enter_context(nc.Block())

        @block.sync
        def _(sp):
            sp.dma_start(xtok[:, 0, :, :], x_v[0, :, :, :]).then_inc(x_loaded[0], 16)

            def load(name, src):
                sp.dma_start(STAGE[name], src.rearrange("(t p) n -> p t n", p=P)).then_inc(w_loaded[name], 16)

            load("wkv", wkv_d)
            load("wq0", wq_d[:, 0:H * D // 2])
            sp.dma_start(kpos[:, :, :], petok_d.rearrange("(n p) d -> p n d", p=P)).then_inc(k_terms_loaded, 16)
            load("wk", wk_d)
            load("wq1", wq_d[:, H * D // 2:H * D])
            load("wr", wr_d)
            load("wv", wv_d)
            for c in range(1, NC):
                sp.dma_start(xtok[:, c, :, :], x_v[c, :, :, :]).then_inc(x_loaded[c], 16)
            for name in ("wq0", "wq1", "wkv", "wk"):
                sp.wait_ge(w_lo[name], 1)
            wo_v = wo_d.rearrange("(t p) n -> p t n", p=P)
            for i, name in enumerate(("wo0", "wo1")):
                sp.dma_start(STAGE[name], wo_v[:, i * H // 2:(i + 1) * H // 2, :]).then_inc(w_loaded[name], 16)

            def store(b, c, t):
                sp.wait_ge(out_ready, b * NT + c * TPC + t + 1)
                sp.dma_start(out_v[bass.ds(b * NT + c * TPC + t, 1), :, :].rearrange("a p e -> (a p) e"),
                             xtok[:, c, t, :]).then_inc(stored[c], 16)

            with sp.Fori(0, B) as b:
                for c in range(NC):
                    for t in range(TPC):
                        store(b, c, t)
                    sp.wait_ge(stored[c], (b + 1) * (16 * TPC))
                    sp.dma_start(xtok[:, c, :, :],
                                 x_v[bass.ds((b * NC + NC + c) % (B * NC), 1), :, :, :]
                                 .rearrange("a p t e -> (a p) t e")).then_inc(x_loaded[c], 16)
            for c in range(NC):
                sp.wait_ge(stored[c], 16 * TPC * B)
                sp.wait_ge(x_loaded[c], 16 * (B + 1))

        @block.gpsimd
        def _(pool):
            nc.gpsimd.memset(ident[:, :], 0.0).then_inc(consts, 1)
            nc.gpsimd.memset(half[:, :], -0.5).then_inc(consts, 1)
            nc.gpsimd.memset(mask[:, :], 0.0).then_inc(consts, 1)
            pool.wait_ge(consts, 3)
            nc.gpsimd.affine_select(out=ident[:, :], in_=ident[:, :], compare_op=ALU.not_equal, fill=1.0,
                                    base=0, pattern=[[-1, P]], channel_multiplier=1).then_inc(consts, 1)
            tri = mask[:, T - P:T]
            nc.gpsimd.affine_select(out=tri, in_=tri, compare_op=ALU.is_ge, fill=MASKED,
                                    base=0, pattern=[[-1, P]], channel_multiplier=1).then_inc(consts, 1)

            def inv_std(n):
                pool.wait_ge(var_ready, n + 1)
                nc.gpsimd.tensor_tensor(rstd[:, :], vare[:, :], half[:, :], ALU.pow).then_inc(rstd_ready, 1)

            def split_xt(n, slot):
                pool.wait_ge(xnt_ready, n + 1)
                nc.gpsimd.tensor_tensor(xt[1][:, slot, :, :], xnt[:, slot, :, 1:CHUNK + 1],
                                        xt[0][:, slot, :, :].bitcast(F), ALU.subtract).then_inc(xt_ready, 1)

            def split_v(n, c):
                pool.wait_ge(v_hi, n + 1)
                tiles = slice(c * TPC, (c + 1) * TPC)
                nc.gpsimd.tensor_tensor(v[1][:, tiles, :], xn[:, :, D:2 * D], v[0][:, tiles, :].bitcast(F),
                                        ALU.subtract).then_inc(v_ready, 1)

            def split_q(n, slot, p, i):
                pool.wait_ge(q_hi, n * PAIRS + p + 1)
                h = 2 * p + i
                nc.gpsimd.tensor_tensor(qt[1][:, slot, h, :], qtmp[:, p % 2, i, :], qt[0][:, slot, h, :].bitcast(F),
                                        ALU.subtract).then_inc(q_ready, 1)

            def split_mix(n, which):
                pool.wait_ge(mix_hi, 2 * n + which + 1)
                nc.gpsimd.tensor_tensor(mh[1][:, :, :], mix[:, :, :], mh[0][:, :, :].bitcast(F),
                                        ALU.subtract).then_inc(mix_split, 1)

            def turn(b, it):
                s = it - 1
                if 0 <= s < STEPS:
                    w = (s // H + 1) * P
                    j = s % XBUF
                    pool.wait_ge(rec_ready, b * STEPS + s + 1)
                    pool.sem_inc(pool_passed, 1)
                    nc.gpsimd.tensor_scalar(X[:, j, 0:w], X[:, j, 0:w], rec[:, j:j + 1], 1.0,
                                            ALU.mult, ALU.mult).then_inc(normed, 1)
                for kind, c, p in FILL[it - 1] if it else []:
                    if kind == "Q":
                        split_q(chunk_no(b, c), c % 2, p, 1)
                c, i = it // PER, it % PER
                if it < STEPS:
                    if i == 2:
                        inv_std(chunk_no(b, c + 1))
                    if i == 2:
                        split_mix(chunk_no(b, c), 1)
                    if i == 4:
                        pool.wait_ge(ka_hi, b * NC + c + 1)
                        nc.gpsimd.tensor_tensor(kh[1][:, :, :], ka[:, :, :], kh[0][:, :, :].bitcast(F),
                                                ALU.subtract).then_inc(ka_split, 1)
                    if i == MIX_AT + 1:
                        split_mix(chunk_no(b, c + 1), 0)
                elif it == STEPS + 4:
                    split_v(chunk_no(b, NC), 0)
                for kind, c, p in FILL[it]:
                    if kind == "XT":
                        split_xt(chunk_no(b, c), c % 2)
                    elif kind == "KV" and c < NC:
                        split_v(chunk_no(b, c), c)
                    elif kind == "Q":
                        split_q(chunk_no(b, c), c % 2, p, 0)

            inv_std(0)
            split_xt(0, 0)
            pool.wait_ge(k_terms_loaded, 32)
            nc.gpsimd.tensor_tensor(kpos[:, :, :], kpos[:, :, :],
                                    bkv[:, 0:D].rearrange("p (a n) -> p a n", a=1).broadcast_to((P, NT, D)),
                                    ALU.add).then_inc(kpos_ready, 1)
            split_v(0, 0)
            split_mix(0, 0)
            for p in range(PAIRS - 1):
                split_q(0, 0, p, 0)
                split_q(0, 0, p, 1)
            for it in range(LEAD):
                turn(0, it)
            with pool.Fori(0, B) as b:
                for it in range(LEAD, STEPS):
                    turn(b, it)
                for it in range(LEAD):
                    turn(b, STEPS + it)
                    turn(b + 1, it)

        @block.scalar
        def _(act):
            act.dma_start(mu[:, :], mu_d).then_inc(mu_loaded, 16)
            act.dma_start(bkv[:, :], bkv_d).then_inc(k_terms_loaded, 16)
            act.dma_start(bq[:, :], bq_d).then_inc(q_terms_loaded, 16)
            act.dma_start(pet[:, :], pet_d).then_inc(q_terms_loaded, 16)

            def weight_hi(name, tiles):
                act.wait_ge(w_loaded[name], 16)
                nc.scalar.copy(W[name][0][:, tiles, :], STAGE[name][:, tiles, :]).then_inc(w_hi[name], 1)

            def xt_out(b, c):
                n = chunk_no(b, c)
                slot = c % 2
                act.wait_ge(filled["XT"], n + 1)
                g = g_bank("XT", c, 0).rearrange("p (t n) -> p t n", t=CT)
                if c % NC:
                    nc.scalar.copy(xnt[:, slot, :, 0:1], xnt[:, 1 - slot, :, CHUNK:CHUNK + 1])
                nc.scalar.copy(xt[0][:, slot, :, :], g)
                nc.scalar.copy(xnt[:, slot, :, 1:CHUNK + 1], g).then_inc(xnt_ready, 1)

            def kt_out(b, c):
                act.wait_ge(filled["KT"], chunk_no(b, c) + 1)
                k0 = (c % NC) * CHUNK
                nc.scalar.activation(kt[0][:, k0:k0 + CHUNK], g_bank("KT", c, 0)[:, 0:CHUNK], ACT.Copy, scale=-1.0
                                     ).then_inc(kt_hi, 1)

            def v_out(b, c):
                act.wait_ge(kv_ready, 2 * chunk_no(b, c) + 2)
                tiles = slice((c % NC) * TPC, (c % NC + 1) * TPC)
                nc.scalar.copy(v[0][:, tiles, :], xn[:, :, D:2 * D]).then_inc(v_hi, 1)

            def q_out(b, c, p):
                act.wait_ge(q_sum, (chunk_no(b, c) * PAIRS + p) * 2 + 2)
                nc.scalar.copy(qt[0][:, c % 2, 2 * p:2 * p + 2, :], qtmp[:, p % 2, :, :]).then_inc(q_hi, 1)

            def mix_before(n, slot, which):
                if which or not isinstance(n, int):
                    act.wait_ge(mix_split, 2 * n + which)
                for t in range(CT):
                    m = (1 - which) * CT + t
                    nc.scalar.activation(mix[:, t, :], xnt[:, slot, t, 0:CHUNK], ACT.Copy,
                                         scale=omu[:, m:m + 1]).then_inc(prev_ready, 1)

            def mix_out(n, which):
                act.wait_ge(mix_ready, (2 * n + which + 1) * CT)
                nc.scalar.copy(mh[0][:, :, :], mix[:, :, :]).then_inc(mix_hi, 1)

            def turn(b, it):
                first = it - PV_LAG
                if 0 <= first < STEPS and first % 2 == 0:
                    pair = first // 2
                    act.wait_ge(pv_done, b * (STEPS // 2) + pair + 1)
                    h = first % H
                    if h == 0 and not (isinstance(b, int) and pair == 0):
                        act.wait_ge(filled["WO"], b * NT + first // H)
                    nc.scalar.copy(ot[0][:, h:h + 2, :],
                                   pO[:, 0:2 * P].rearrange("p (h q) -> p h q", h=2)).then_inc(o_hi, 1)
                s = it - T_LAG
                if 0 <= s < STEPS:
                    half_q = slice((s % 2) * P, (s % 2 + 1) * P)
                    for m, (k, nk) in enumerate(t_banks(s)):
                        u = T_FIRST[s] + m
                        act.wait_ge(t_filled, b * T_BODY + u + 1)
                        nc.scalar.copy(pt[0][:, (s // 2) % 2, k:k + nk, half_q],
                                       pT[u % 2][:, 0:nk * P].rearrange("p (k q) -> p k q", k=nk)
                                       ).then_inc(t_hi, 1)
                s = it - 1
                if 0 <= s < STEPS:
                    w = (s // H + 1) * P
                    j = s % XBUF
                    act.wait_ge(masked, b * STEPS + s + 1)
                    nc.scalar.activation(X[:, j, 0:w], X[:, j, 0:w], ACT.Exp, bias=bias[:, j:j + 1],
                                         scale=-1.0, accum_out=total[:, j:j + 1]).then_inc(exp_done, 1)
                for kind, c, p in FILL[it]:
                    if kind == "XT":
                        xt_out(b, c)
                    elif kind == "KT":
                        if c == NC:
                            act.wait_ge(s_filled, (b + 1) * STEPS)
                        kt_out(b, c)
                    elif kind == "KV" and c < NC:
                        v_out(b, c)
                    elif kind == "FK":
                        act.wait_ge(filled["FK"], b * NC + c + 1)
                        nc.scalar.activation(ka[:, :, :], g_bank(kind, c, p).rearrange("p (t n) -> p t n", t=CT),
                                             ACT.Relu).then_inc(relu_ready, 1)
                        act.wait_ge(relu_ready, b * NC + c + 1)
                        nc.scalar.activation(ka[:, :, :], ka[:, :, :], ACT.Square).then_inc(square_ready, 1)
                    elif kind == "FR":
                        act.wait_ge(filled["FR"], b * NC + c + 1)
                        nc.scalar.activation(gate[:, :, :], g_bank(kind, c, p).rearrange("p (t n) -> p t n", t=TPC),
                                             ACT.Tanh, scale=0.5).then_inc(tanh_ready, 1)
                    elif kind == "Q":
                        q_out(b, c, p)
                c, i = it // PER, it % PER
                if it < STEPS:
                    if i == 0:
                        mix_before(chunk_no(b, c), c % 2, 1)
                    if i == MIX_AT - 1:
                        act.wait_ge(xnt_ready, chunk_no(b, c + 1) + 1)
                        if c == NC - 1:
                            act.wait_ge(xnt_zero, b + 2)
                        mix_before(chunk_no(b, c + 1), (c + 1) % 2, 0)
                    if i == 2:
                        mix_out(chunk_no(b, c), 1)
                    if i == 4:
                        act.wait_ge(square_ready, b * NC + c + 1)
                        nc.scalar.copy(kh[0][:, :, :], ka[:, :, :]).then_inc(ka_hi, 1)
                    if i == MIX_AT + 1:
                        act.wait_ge(filled["FR"], b * NC + c + 1)
                        mix_out(chunk_no(b, c + 1), 0)
                elif it == STEPS + 4:
                    act.wait_ge(pv_done, (b + 1) * (STEPS // 2))
                    v_out(b, NC)

            weight_hi("wkv", slice(0, CT))
            xt_out(None, 0)
            act.wait_ge(xnt_ready, 1)
            act.wait_ge(xnt_zero, 1)
            act.wait_ge(omu_ready, 1)
            mix_before(0, 0, 0)
            weight_hi("wq0", slice(0, CT))
            weight_hi("wq1", slice(0, CT))
            kt_out(None, 0)
            v_out(None, 0)
            mix_out(0, 0)
            weight_hi("wk", slice(0, CT))
            for p in range(PAIRS - 1):
                q_out(None, 0, p)
            for it in range(LEAD):
                turn(0, it)
                if it in LATE:
                    weight_hi(*LATE[it])
            with act.Fori(0, B) as b:
                for it in range(LEAD, STEPS):
                    turn(b, it)
                for it in range(LEAD):
                    turn(b, STEPS + it)
                    turn(b + 1, it)

        @block.vector
        def _(dve):
            def norm_stats(n, slot, b):
                dve.wait_ge(x_loaded[slot], 16 if b is None else 16 * ((b + 1) if slot else (b + 2)))
                for t in range(TPC):
                    nc.vector.bn_stats(stats[:, t, :], xtok[:, slot, t, :]).then_inc(bn_done, 1)
                dve.wait_ge(bn_done, n * 2 * TPC + TPC)
                dve.sem_inc(dve_passed, 1)
                for t in range(TPC):
                    nc.vector.bn_aggr(mv[:, t, :], stats[:, t, :]).then_inc(bn_done, 1)
                dve.wait_ge(bn_done, n * 2 * TPC + 2 * TPC)
                nc.vector.tensor_scalar_add(vare[:, :], mv[:, :, 1], EPS).then_inc(var_ready, 1)

            def norm_apply(n, slot):
                dve.wait_ge(rstd_ready, n + 1)
                for t in range(TPC):
                    nc.vector.tensor_scalar(xn[:, t, :], xtok[:, slot, t, :], mv[:, t, 0:1], rstd[:, t:t + 1],
                                            ALU.subtract, ALU.mult).then_inc(xn_ready, 1)

            def kv_out(b, c):
                n = chunk_no(b, c)
                dve.wait_ge(filled["KV"], chunk_no(b, c) + 1)
                g = g_bank("KV", c, 0).rearrange("p (t n) -> p t n", t=TPC)
                tiles = slice((c % NC) * TPC, (c % NC + 1) * TPC)
                nc.vector.tensor_tensor(xn[:, :, 0:D], g[:, :, 0:D], kpos[:, tiles, :], ALU.add
                                        ).then_inc(kv_ready, 1)
                nc.vector.tensor_tensor(xn[:, :, D:2 * D], g[:, :, D:2 * D],
                                        bkv[:, D:2 * D].rearrange("p (a n) -> p a n", a=1).broadcast_to((P, TPC, D)),
                                        ALU.add).then_inc(kv_ready, 1)

            def kt_out(b, c):
                dve.wait_ge(kt_hi, chunk_no(b, c) + 1)
                k0 = (c % NC) * CHUNK
                nc.vector.scalar_tensor_tensor(kt[1][:, k0:k0 + CHUNK], g_bank("KT", c, 0)[:, 0:CHUNK], -1.0,
                                               kt[0][:, k0:k0 + CHUNK].bitcast(F), ALU.mult, ALU.subtract
                                               ).then_inc(kt_ready, 1)

            def q_out(b, c, p):
                n = chunk_no(b, c)
                dve.wait_ge(filled["Q"], chunk_no(b, c) * PAIRS + p + 1)
                if b is not None or p > 1:
                    dve.wait_ge(q_ready, 2 * (n * PAIRS + p - 1))
                t0 = (c % NC) * CHUNK
                for i in range(2):
                    h = 2 * p + i
                    nc.vector.scalar_tensor_tensor(qtmp[:, p % 2, i, :],
                                                   g_bank("Q", c, p)[:, i * CHUNK:(i + 1) * CHUNK], bq[:, h:h + 1],
                                                   pet[:, t0:t0 + CHUNK], ALU.add, ALU.add).then_inc(q_sum, 1)

            def token_mix(n, slot, which):
                n = 2 * n + which
                x_now = xnt[:, slot, :, 1:CHUNK + 1]
                dve.wait_ge(prev_ready, n * CT + CT)
                for t in range(CT):
                    m = (1 - which) * CT + t
                    nc.vector.scalar_tensor_tensor(mix[:, t, :], x_now[:, t, :], mu[:, m:m + 1], mix[:, t, :],
                                                   ALU.mult, ALU.add).then_inc(mix_ready, 1)

            norm_stats(0, 0, None)
            nc.vector.memset(xnt[:, 0, :, 0:1], 0.0).then_inc(xnt_zero, 1)
            norm_apply(0, 0)
            def weight_lo(name, tiles, done=1):
                dve.wait_ge(w_hi[name], done)
                nc.vector.tensor_tensor(W[name][1][:, tiles, :], STAGE[name][:, tiles, :],
                                        W[name][0][:, tiles, :].bitcast(F), ALU.subtract).then_inc(w_lo[name], 1)

            weight_lo("wkv", slice(0, CT))
            dve.wait_ge(mu_loaded, 16)
            nc.vector.tensor_scalar(omu[:, :], mu[:, :], -1.0, 1.0, ALU.mult, ALU.add).then_inc(omu_ready, 1)
            weight_lo("wq0", slice(0, CT))
            weight_lo("wq1", slice(0, CT))
            dve.wait_ge(kpos_ready, 1)
            kv_out(None, 0)
            token_mix(0, 0, 0)
            kt_out(None, 0)
            dve.wait_ge(q_terms_loaded, 32)
            q_out(None, 0, 0)
            weight_lo("wk", slice(0, CT))
            q_out(None, 0, 1)
            q_out(None, 0, 2)
            dve.wait_ge(consts, 5)

            def turn(b, it):
                first_row = isinstance(b, int)
                first = it - PV_LAG
                if 0 <= first < STEPS and first % 2 == 0:
                    pair = first // 2
                    dve.wait_ge(o_hi, b * (STEPS // 2) + pair + 1)
                    h = first % H
                    nc.vector.tensor_tensor(ot[1][:, h:h + 2, :],
                                            pO[:, 0:2 * P].rearrange("p (h q) -> p h q", h=2),
                                            ot[0][:, h:h + 2, :].bitcast(F), ALU.subtract).then_inc(o_lo, 1)
                s = it - T_LAG
                if 0 <= s < STEPS:
                    half_q = slice((s % 2) * P, (s % 2 + 1) * P)
                    for m, (k, nk) in enumerate(t_banks(s)):
                        u = T_FIRST[s] + m
                        dve.wait_ge(t_hi, b * T_BODY + u + 1)
                        nc.vector.tensor_tensor(pt[1][:, (s // 2) % 2, k:k + nk, half_q],
                                                pT[u % 2][:, 0:nk * P].rearrange("p (k q) -> p k q", k=nk),
                                                pt[0][:, (s // 2) % 2, k:k + nk, half_q].bitcast(F),
                                                ALU.subtract).then_inc(t_lo, 1)
                for kind, c, p in FILL[it]:
                    n = chunk_no(b, c)
                    if kind == "XT":
                        if c == NC:
                            nc.vector.memset(xnt[:, 0, :, 0:1], 0.0).then_inc(xnt_zero, 1)
                    elif kind == "KV":
                        kv_out(b, c)
                    elif kind == "KT":
                        kt_out(b, c)
                    elif kind == "Q":
                        q_out(b, c, p)
                    elif kind == "FV":
                        dve.wait_ge(tanh_ready, n + 1)
                        dve.wait_ge(filled["FV"], n + 1)
                        nc.vector.scalar_tensor_tensor(gate[:, :, :], gate[:, :, :], 1.0,
                                                       g_bank(kind, c, p).rearrange("p (t n) -> p t n", t=TPC),
                                                       ALU.add, ALU.mult).then_inc(gated_ready, 1)
                        dve.wait_ge(gated_ready, n + 1)
                        nc.vector.scalar_tensor_tensor(xtok[:, c, :, :], gate[:, :, :], 0.5, xtok[:, c, :, :],
                                                       ALU.mult, ALU.add).then_inc(mixed, 1)
                    elif kind == "WO":
                        dve.wait_ge(mixed, n + 1)
                        dve.wait_ge(filled["WO"], b * NT + c * TPC + p + 1)
                        nc.vector.tensor_tensor(xtok[:, c, p, :], g_bank(kind, c, p)[:, 0:E], xtok[:, c, p, :], ALU.add
                                                ).then_inc(out_ready, 1)
                c, i = it // PER, it % PER
                if it < STEPS:
                    n = chunk_no(b, c)
                    if i == 2:
                        norm_stats(chunk_no(b, c + 1), (c + 1) % NC, b)
                    elif i == 1:
                        token_mix(n, c % 2, 1)
                    elif i == 5:
                        dve.wait_ge(v_ready, n + 1)
                        dve.wait_ge(filled["KT"], n + 1)
                        norm_apply(chunk_no(b, c + 1), (c + 1) % NC)
                    elif i == MIX_AT:
                        n = chunk_no(b, c + 1)
                        token_mix(n, (c + 1) % 2, 0)
                s = it
                if s < STEPS:
                    qi = s // H
                    w = (qi + 1) * P
                    j = s % XBUF
                    if qi < 4:
                        scores = pS[s % 2][:, 0, 0:w]
                        m = mask[:, T - w:T]
                        o = X[:, j, 0:w]
                    else:
                        scores = pS[s % 2][:, :, 0:w // 2]
                        m = mask[:, T - w:T].rearrange("p (a n) -> p a n", a=2)
                        o = X[:, j, 0:w].rearrange("p (a n) -> p a n", a=2)
                    if s >= XBUF:
                        dve.wait_ge(t_filled, b * T_BODY + T_FIRST[s - XBUF + 1])
                    elif not first_row:
                        dve.wait_ge(t_filled, (b - 1) * T_BODY + T_FIRST[STEPS + s - XBUF + 1])
                    dve.wait_ge(s_filled, b * STEPS + s + 1)
                    dve.sem_inc(dve_passed, 1)
                    nc.vector.tensor_tensor_reduce(out=o, in0=scores, in1=m, scale=SCALE, scalar=HUGE,
                                                   op0=ALU.add, op1=ALU.min,
                                                   accum_out=bias[:, j:j + 1]).then_inc(masked, 1)
                s = it - 1
                if 0 <= s < STEPS:
                    j = s % XBUF
                    dve.wait_ge(exp_done, b * STEPS + s + 1)
                    nc.vector.reciprocal(rec[:, j:j + 1], total[:, j:j + 1]).then_inc(rec_ready, 1)

            for it in range(LEAD):
                turn(0, it)
                if it in LATE:
                    name, tiles = LATE[it]
                    weight_lo(name, tiles, len([x for i, x in LATE.items() if i <= it and x[0] == name]))
            with dve.Fori(0, B) as b:
                for it in range(LEAD, STEPS):
                    turn(b, it)
                for it in range(LEAD):
                    turn(b, STEPS + it)
                    turn(b + 1, it)

        @block.tensor
        def _(pe):
            PASSES = ((0, 0), (0, 1), (1, 0))

            def product(out, terms, start=True):
                n = len(terms) * len(PASSES)
                k = 0
                for a, m in terms:
                    for i, j in PASSES:
                        last = nc.tensor.matmul(out, a[i], m[j], start=start and k == 0, stop=k == n - 1)
                        k += 1
                return last

            def wait_emptied(b, u):
                kind, c, p = u
                n = chunk_no(b, c)
                if kind == "XT":
                    pe.wait_ge(xnt_ready, n + 1)
                elif kind == "KV":
                    pe.wait_ge(kv_ready, 2 * n + 2)
                elif kind == "KT":
                    pe.wait_ge(kt_ready, n + 1)
                elif kind == "Q":
                    pe.wait_ge(q_sum, (n * PAIRS + p) * 2 + 2)
                elif kind == "FK":
                    pe.wait_ge(relu_ready, n + 1)
                elif kind == "FR":
                    pe.wait_ge(tanh_ready, n + 1)
                elif kind == "FV":
                    pe.wait_ge(gated_ready, n + 1)
                else:
                    pe.wait_ge(out_ready, b * NT + c * TPC + p + 1)

            def fill(b, u, row, place):
                kind, c, p = u
                out = g_bank(kind, c, p)
                if row is None:
                    k = [x for _, x in G_FIRST].index(u)
                    found = used_before(G_FIRST, k)
                    if found and found[0] >= 0:
                        wait_emptied(*found[1])
                else:
                    found, (rows, before) = used_before(G_ORDER, G_ORDER.index((place, u)))
                    if found >= 0 or rows:
                        wait_emptied(row + rows - (found < 0), before)
                n = chunk_no(b, c)
                slot = c % 2
                if kind == "XT":
                    pe.wait_ge(xn_ready, n * TPC + TPC)
                    for ct in range(CT):
                        for t in range(TPC):
                            o = ct * CHUNK + t * P
                            last = nc.tensor.transpose(out[:, o:o + P], xn[:, t, ct * P:(ct + 1) * P], ident[:, :])
                elif kind == "KV":
                    pe.wait_ge(xt_ready, n + 1)
                    for t in range(TPC):
                        last = product(out[:, t * 2 * D:(t + 1) * 2 * D],
                                       [([x[:, slot, ct, t * P:(t + 1) * P] for x in xt],
                                         [w[:, ct, :] for w in wkv]) for ct in range(CT)])
                elif kind == "KT":
                    pe.wait_ge(kv_ready, 2 * n + 2)
                    for t in range(TPC):
                        last = nc.tensor.transpose(out[:, t * P:(t + 1) * P], xn[:, t, 0:D], ident[:, :])
                elif kind == "Q":
                    for i in range(2):
                        h = 2 * p + i
                        last = product(out[:, i * CHUNK:(i + 1) * CHUNK],
                                       [([w[:, ct, h * D:(h + 1) * D] for w in wq],
                                         [x[:, slot, ct, :] for x in xt]) for ct in range(CT)])
                elif kind == "FK":
                    pe.wait_ge(mix_split, (b * NC + c) * 2 + 1)
                    for j in range(CT):
                        last = product(out[:, j * CHUNK:(j + 1) * CHUNK],
                                       [([w[:, ct, j * P:(j + 1) * P] for w in wk],
                                         [m[:, ct, :] for m in mh]) for ct in range(CT)])
                elif kind == "FR":
                    pe.wait_ge(mix_split, (b * NC + c) * 2 + 2)
                    for t in range(TPC):
                        last = product(out[:, t * E:(t + 1) * E],
                                       [([m[:, ct, t * P:(t + 1) * P] for m in mh],
                                         [w[:, ct, :] for w in wr]) for ct in range(CT)])
                elif kind == "FV":
                    pe.wait_ge(ka_split, b * NC + c + 1)
                    for t in range(TPC):
                        last = product(out[:, t * E:(t + 1) * E],
                                       [([m[:, ct, t * P:(t + 1) * P] for m in kh],
                                         [w[:, ct, :] for w in wv]) for ct in range(CT)])
                elif kind == "WO":
                    pe.wait_ge(o_lo, (b * NT + c * TPC + p + 1) * PAIRS)
                    last = product(out[:, 0:E], [([o[:, h, :] for o in ot], [w[:, h, :] for w in wo])
                                                for h in range(H)])
                last.then_inc(filled[kind], 1)

            def turn(b, it, row=None, place=0):
                first_row = isinstance(b, int)
                first = it - PV_LAG
                if 0 <= first < STEPS and first % 2 == 0:
                    pair = first // 2
                    nk = first // H + 1
                    if first % PER == 0:
                        pe.wait_ge(v_ready, b * NC + first // PER + 1)
                    if pair or not first_row:
                        pe.wait_ge(o_lo, b * (STEPS // 2) + pair)
                    pe.wait_ge(t_lo, b * T_BODY + T_FIRST[first + 2])
                    last = product(pO[:, 0:2 * P],
                                   [([x[:, k, :] for x in v], [x[:, pair % 2, k, :] for x in pt])
                                    for k in range(nk)])
                    last.then_inc(pv_done, 1)
                s = it - T_LAG
                if 0 <= s < STEPS:
                    pe.wait_ge(normed, b * STEPS + s + 1)
                    for m, (k, nk) in enumerate(t_banks(s)):
                        u = T_FIRST[s] + m
                        if u >= 2 or not first_row:
                            pe.wait_ge(t_lo, b * T_BODY + u - 1)
                        for i in range(nk):
                            last = nc.tensor.transpose(pT[u % 2][:, i * P:(i + 1) * P],
                                                       X[:, s % XBUF, (k + i) * P:(k + i + 1) * P],
                                                       ident[:, :])
                        last.then_inc(t_filled, 1)
                for u in FILL[it]:
                    fill(b, u, row, place)
                s = it
                if s < STEPS:
                    qi, h = s // H, s % H
                    c, t = qi // TPC, qi % TPC
                    w = (qi + 1) * P
                    n = chunk_no(b, c)
                    if s % PER == 0:
                        pe.wait_ge(kt_ready, n + 1)
                    if t == 0:
                        pe.wait_ge(q_ready, n * H + h + 1)
                    if s >= 2 or not first_row:
                        pe.wait_ge(masked, b * STEPS + s - 1)
                    if SHARED <= s < SHARED + 2:
                        wait_emptied(b, [u for it in range(SHARED) for u in FILL[it]
                                         if G_BANK[u] == s - SHARED + 1][-1])
                    halves = 1 if qi < 4 else 2
                    wn = w // halves
                    for a in range(halves):
                        last = product(pS[s % 2][:, a, 0:wn],
                                       [([q[:, c % 2, h, t * P:(t + 1) * P] for q in qt],
                                         [k[:, a * wn:(a + 1) * wn] for k in kt])])
                    last.then_inc(s_filled, 1)

            pe.wait_ge(consts, 5)
            fill(None, START[0], None, 0)
            pe.wait_ge(w_lo["wkv"], 1)
            for u in START[1:]:
                if u[0] == "Q" and u[2] % 2 == 0:
                    pe.wait_ge(w_lo[f"wq{u[2] // 2}"], 1)
                fill(None, u, None, 0)
            pe.wait_ge(w_lo["wk"], 1)
            for it in range(LEAD):
                if ("FR", 0, 0) in FILL[it]:
                    pe.wait_ge(w_lo["wr"], 1)
                turn(0, it)
            pe.wait_ge(w_lo["wv"], 1)
            pe.wait_ge(w_lo["wo0"], 2)
            pe.wait_ge(w_lo["wo1"], 2)
            with pe.Fori(0, B) as b:
                for it in range(LEAD, STEPS):
                    turn(b, it, b, 0)
                for it in range(LEAD):
                    turn(b, STEPS + it, b, 0)
                    turn(b + 1, it, b, 1)


def _positions():
    import numpy as np
    pos = np.arange(T, dtype=np.float32)[:, None]
    inv = np.exp(np.float32(-np.log(10000.0)) * np.arange(0, D, 2, dtype=np.float32) / np.float32(D))
    ang = (pos * inv.astype(np.float32)[None, :]).astype(np.float32)
    pe = np.zeros((T, D), np.float32)
    pe[:, 0::2] = np.sin(ang)
    pe[:, 1::2] = np.cos(ang)
    return pe


def kernel(L0_attn_x, L0_attn_Wq, L0_attn_bq, L0_attn_Wkv, L0_attn_bkv, L0_attn_Wo, L0_ffn_W_r, L0_ffn_W_k,
           L0_ffn_W_v, L0_ffn_mu_r, L0_ffn_mu_k):
    import numpy as np
    import concourse.bacc as bacc
    from concourse.bass_utils import run_bass_kernel_spmd

    pe = _positions()
    arrays = {
        "x": np.asarray(L0_attn_x),
        "wq": np.asarray(L0_attn_Wq),
        "wkv": np.asarray(L0_attn_Wkv),
        "wo": np.asarray(L0_attn_Wo),
        "wr": np.asarray(L0_ffn_W_r).T,
        "wk": np.asarray(L0_ffn_W_k).T,
        "wv": np.asarray(L0_ffn_W_v).T,
        "bq": np.asarray(L0_attn_bq).reshape(H, D).T,
        "bkv": np.tile(np.asarray(L0_attn_bkv)[None, :], (P, 1)),
        "mu": np.concatenate([np.asarray(L0_ffn_mu_r).reshape(CT, P), np.asarray(L0_ffn_mu_k).reshape(CT, P)]).T,
        "pet": pe.T,
        "petok": pe,
    }
    arrays = {name: np.ascontiguousarray(a) for name, a in arrays.items()}
    nc = bacc.Bacc("TRN2", target_bir_lowering=False, num_devices=1)
    args = [nc.dram_tensor(name + "_dram", a.shape, mybir.dt.from_np(a.dtype), kind="ExternalInput").ap()
            for name, a in arrays.items()]
    out = nc.dram_tensor("out_dram", (B, T, E), mybir.dt.float32, kind="ExternalOutput").ap()
    build(nc, *args, out)
    r = run_bass_kernel_spmd(nc, [{name + "_dram": a for name, a in arrays.items()}], core_ids=[0])
    return r.results[0]["out_dram"]
```
